# Optimizing a Trainium2 kernel written in Bass

```python
import numpy as np
import jax
import jax.numpy as jnp

def _softmax(x, axis=-1):
    return jax.nn.softmax(x, axis=axis)

def _gelu(x):
    return jax.nn.gelu(x, approximate=True)

def _silu(x):
    return jax.nn.silu(x)

def _sigmoid(x):
    return jax.nn.sigmoid(x)

def _layernorm(x, axis=-1, eps=1e-05):
    m = jnp.mean(x, axis=axis, keepdims=True)
    v = jnp.var(x, axis=axis, keepdims=True)
    return (x - m) / jnp.sqrt(v + eps)

def _scatter_add(tgt, idx, src, axis=0):
    return tgt.at[idx].add(src)

def _segment_sum(src, seg, n):
    return jax.ops.segment_sum(src, seg, n)
kernel_name = 'mk_rec_standalone_d1_rec_r8_1f0f46'

def setup_inputs(seed: int=0):
    np.random.seed(seed)
    _w = jnp.asarray

    def _rec_inputs():
        import jax
        import jax.numpy as jnp
        _rk = jax.random.key(seed)
        r_hist_items = -0.000161372 + 0.999968 * jax.random.normal(jax.random.fold_in(_rk, 1), (512, 200, 128), jnp.float32)
        r_hist_mask = jax.random.bernoulli(jax.random.fold_in(_rk, 2), 0.5013, (512, 200))
        r_hist_age_hours = jax.random.uniform(jax.random.fold_in(_rk, 3), (512, 200), jnp.float32, 0.0, 168)
        r_hist_popularity = jax.random.uniform(jax.random.fold_in(_rk, 4), (512, 200), jnp.float32, 0.0, 0.999999)
        return (r_hist_items, r_hist_mask, r_hist_age_hours, r_hist_popularity)
    r_hist_items, r_hist_mask, r_hist_age_hours, r_hist_popularity = _rec_inputs()

    def _L0_rec_setup():
        import jax, jax.numpy as jnp
        import numpy as np
        B, T, D = (512, 200, 128)
        K_SHORT = 5
        key = jax.random.key(seed)
        ks = jax.random.split(key, 8)
        hist_items = jax.random.normal(ks[0], (B, T, D), dtype=jnp.float32)
        hist_mask = jax.random.randint(ks[1], (B, T), 0, 2).astype(bool)
        hist_mask = hist_mask.at[:, 0].set(True)
        hist_age_hours = jax.random.uniform(ks[2], (B, T), dtype=jnp.float32) * 168.0
        hist_popularity = jax.random.uniform(ks[3], (B, T), dtype=jnp.float32)
        s = 1.0 / float(np.sqrt(D))
        Wq = jax.random.normal(ks[4], (D, D), dtype=jnp.float32) * s
        Wk = jax.random.normal(ks[5], (D, D), dtype=jnp.float32) * s
        Wv = jax.random.normal(ks[6], (D, D), dtype=jnp.float32) * s
        gate_w = jax.random.normal(ks[7], (1, 2), dtype=jnp.float32) * 0.5
        gate_b = jnp.zeros((1,), dtype=jnp.float32)
        ln_gamma = jnp.ones((D,), dtype=jnp.float32)
        ln_beta = jnp.zeros((D,), dtype=jnp.float32)
        decay_alpha = jnp.asarray(0.05, dtype=jnp.float32)
        return {'hist_items': hist_items, 'hist_mask': hist_mask, 'hist_age_hours': hist_age_hours, 'hist_popularity': hist_popularity, 'Wq': Wq, 'Wk': Wk, 'Wv': Wv, 'gate_w': gate_w, 'gate_b': gate_b, 'ln_gamma': ln_gamma, 'ln_beta': ln_beta, 'decay_alpha': decay_alpha}
    _L0_rec_all = _L0_rec_setup()
    _L0_rec_in = {k: v for k, v in _L0_rec_all.items() if k in ('Wq', 'Wk', 'Wv', 'gate_w', 'gate_b', 'ln_gamma', 'ln_beta', 'decay_alpha')}
    del _L0_rec_all
    return {'r_hist_items': r_hist_items, 'r_hist_mask': r_hist_mask, 'r_hist_age_hours': r_hist_age_hours, 'r_hist_popularity': r_hist_popularity, 'L0_rec_Wq': _L0_rec_in['Wq'], 'L0_rec_Wk': _L0_rec_in['Wk'], 'L0_rec_Wv': _L0_rec_in['Wv'], 'L0_rec_gate_w': _L0_rec_in['gate_w'], 'L0_rec_gate_b': _L0_rec_in['gate_b'], 'L0_rec_ln_gamma': _L0_rec_in['ln_gamma'], 'L0_rec_ln_beta': _L0_rec_in['ln_beta'], 'L0_rec_decay_alpha': _L0_rec_in['decay_alpha']}

def reference(r_hist_items, r_hist_mask, r_hist_age_hours, r_hist_popularity, L0_rec_Wq, L0_rec_Wk, L0_rec_Wv, L0_rec_gate_w, L0_rec_gate_b, L0_rec_ln_gamma, L0_rec_ln_beta, L0_rec_decay_alpha):
    import jax
    import jax.numpy as jnp

    def _L0_rec_ref(hist_items, hist_mask, hist_age_hours, hist_popularity, Wq, Wk, Wv, gate_w, gate_b, ln_gamma, ln_beta, decay_alpha):
        import jax, jax.numpy as jnp
        import numpy as np
        B, T, D = (512, 200, 128)
        K_SHORT = 5
        dt = hist_items.dtype
        maskf = hist_mask.astype(dt)
        alpha = jax.nn.softplus(decay_alpha) + 1e-06
        decay = jnp.exp(-alpha * hist_age_hours) * maskf
        mean_hist = (hist_items * maskf[..., None]).sum(1) / (maskf.sum(1, keepdims=True) + 1e-06)
        q = mean_hist @ Wq.T
        k = jnp.einsum('btd,ed->bte', hist_items, Wk)
        v = jnp.einsum('btd,ed->bte', hist_items, Wv)
        scale = 1.0 / float(np.sqrt(hist_items.shape[-1]))
        scores = jnp.einsum('bd,btd->bt', q, k) * scale + jnp.log(decay + 1e-12)
        scores = jnp.where(hist_mask, scores, -jnp.inf)
        attn = jax.nn.softmax(scores, axis=-1)
        long_term = jnp.einsum('bt,btd->bd', attn, v)
        cnt = jnp.maximum(hist_mask.sum(1), 1)
        K = min(K_SHORT, hist_items.shape[1])
        ar = jnp.arange(hist_items.shape[1])[None, :]
        lastk = (ar >= cnt[:, None] - K) & (ar < cnt[:, None])
        lk = lastk.astype(dt)
        denom = jnp.maximum(lk.sum(1, keepdims=True), 1.0)
        short_term = (hist_items * lk[..., None]).sum(1) / denom
        mean_pop = (hist_popularity * lk).sum(1) / denom[:, 0]
        mean_rec = (hist_age_hours * lk).sum(1) / denom[:, 0]
        ctx = jnp.stack([mean_pop, mean_rec], axis=-1)
        g = jax.nn.sigmoid(ctx @ gate_w.T + gate_b)
        user = g * short_term + (1.0 - g) * long_term
        mu = user.mean(-1, keepdims=True)
        var = user.var(-1, keepdims=True)
        return (user - mu) / jnp.sqrt(var + 1e-05) * ln_gamma + ln_beta
    y = _L0_rec_ref(r_hist_items, r_hist_mask, r_hist_age_hours, r_hist_popularity, L0_rec_Wq, L0_rec_Wk, L0_rec_Wv, L0_rec_gate_w, L0_rec_gate_b, L0_rec_ln_gamma, L0_rec_ln_beta, L0_rec_decay_alpha)
    return y

_drawn_inputs = setup_inputs


def setup_inputs(seed=0):
    import zlib

    import numpy as np

    out = dict(_drawn_inputs(seed))
    spreads = {'L0_rec_ln_gamma': (1.0, 0.2), 'L0_rec_ln_beta': (0.0, 0.1)}
    factors = {'r_hist_popularity': 64.0, 'L0_rec_gate_w': 8.0}
    for name, (base, spread) in spreads.items():
        noise = np.random.default_rng([zlib.crc32(name.encode()), seed]).standard_normal(out[name].shape)
        drawn = base * np.exp(spread * noise) if base else spread * noise
        out[name] = jnp.asarray(drawn.astype(out[name].dtype))
    for name, factor in factors.items():
        out[name] = (out[name] * factor).astype(out[name].dtype)
    return out
```

```python
import concourse.bass as bass
from concourse import mybir
from concourse.alu_op_type import AluOpType as ALU
from contextlib import ExitStack

F32 = mybir.dt.float32
U8 = mybir.dt.uint8
I32 = mybir.dt.int32
U32 = mybir.dt.uint32
ACT = mybir.ActivationFunctionType
AX = mybir.AxisListType

NUSER, NITEM, D = 512, 200, 128
P = 128
LAST = 5
PU = 8
ROWS = NITEM // PU
TU = P // PU
NTILE = NUSER // TU
PAIR = 2
NPAIR = NTILE // PAIR
GP = 4
NGROUP = NPAIR // GP
SLOTS = GP * PAIR
PROWS = PAIR * ROWS
PUSERS = PAIR * TU
NPROD = (ROWS + 1) // 2
BIG = 3.0e38
SCALE = float(D) ** -0.5

DOTS = 14
VPROD = 3
GPROD = ROWS - DOTS - VPROD
GCHUNKS = ((0, GPROD // 2), (GPROD // 2, GPROD))
POOL_IDENT = 5
POOL_CONSTANTS = 17


def build(nc, items, mask, age, pop, Wq, Wk, Wv, gate_w, gate_b, gamma, beta, decay_alpha, out):
    items_t = items.rearrange("u t d -> (u t d)").rearrange("(g p n) -> g p n", p=P, n=ROWS * D)
    items_rows = items.rearrange("u t d -> (u t) d")
    mask_t = mask.rearrange("u t -> (u t)").rearrange("(g p r) -> p g r", p=P, r=ROWS)
    age_t = age.rearrange("u t -> (u t)").rearrange("(g p r) -> p g r", p=P, r=ROWS)
    mask_pairs = mask.rearrange("(s u) t -> u s t", u=PUSERS)
    mask_n, age_n, pop_n = (a.rearrange("(q u) t -> u q t", u=P) for a in (mask, age, pop))

    ctx = ExitStack()
    with ctx:
        def sb(name, shape, dt=F32):
            return ctx.enter_context(nc.sbuf_tensor(name, shape, dt))

        def bank(name):
            return ctx.enter_context(nc.psum_tensor(name, [P, 512], F32))

        def sem(name):
            return ctx.enter_context(nc.semaphore(name))

        x = sb("x", [P, SLOTS, ROWS * D])
        wq, wk, wv = sb("wq", [P, D]), sb("wk", [P, D]), sb("wv", [P, D])
        wqk, wv_t = sb("wqk", [P, D]), sb("wv_t", [P, D])
        ident = sb("ident", [P, P])
        ones = sb("ones", [P, 1])
        own = sb("own", [P, TU])
        fold = sb("fold", [P, 2, PAIR, TU])
        spread = sb("spread", [PUSERS, PAIR * P])
        gam, bet = sb("gam", [P, D]), sb("bet", [P, D])
        gw, gb, da = sb("gw", [P, 2]), sb("gb", [P, 1]), sb("da", [P, 1])
        mask_p = sb("mask_p", [P, NTILE, ROWS], U8)
        mask_f = sb("mask_f", [P, NTILE, ROWS])
        mask_s = sb("mask_s", [PUSERS, NPAIR, NITEM], U8)
        mask_u = sb("mask_u", [P, NGROUP, NITEM], U8)
        age_p = sb("age_p", [P, NTILE * ROWS])
        decay = sb("decay", [P, NTILE * ROWS])
        hide = sb("hide", [P, NTILE * ROWS])
        age_u, pop_u = sb("age_u", [P, NGROUP, NITEM]), sb("pop_u", [P, NGROUP, NITEM])
        pos = sb("pos", [P, NITEM])
        rcnt = sb("rcnt", [PUSERS, NPAIR])
        st = sb("st", [P, 16, NGROUP])
        soft = sb("soft", [P, 8])
        stay_ = sb("stay", [P, NGROUP])
        last = sb("last", [P, 2, NITEM])
        junk_u = sb("junk_u", [P, NITEM])
        junk_v = sb("junk_v", [P, PAIR, DOTS, D])
        junk_a = sb("junk_a", [P, PAIR, ROWS - DOTS, D])
        first_row = sb("first_row", [P, NGROUP], U32)
        user0 = sb("user0", [P, NGROUP])
        taken = sb("taken", [P, NGROUP, LAST, D])
        lw = sb("lw", [P, LAST, NGROUP])
        short = sb("short", [P, NGROUP, D])
        mblk = sb("mblk", [P, 2, PAIR, ROWS, TU])
        pblk = sb("pblk", [P, 2, PAIR, ROWS, TU])
        sums = sb("sums", [P, 2 * D])
        mean = sb("mean", [PUSERS, D])
        mean_p = sb("mean_p", [P, PAIR * P])
        query = sb("query", [P, 2, PAIR, D])
        gprod = sb("gprod", [P, PAIR, GPROD * D])
        score = sb("score", [P, 2, PAIR, ROWS])
        kept = sb("kept", [P, PROWS])
        pmax = sb("pmax", [P, PAIR])
        umax = sb("umax", [PAIR, TU])
        nmax = sb("nmax", [PAIR, P])
        nmax_p = sb("nmax_p", [P, PAIR])
        ex = sb("ex", [P, PAIR, ROWS])
        wts = sb("wts", [P, PAIR, ROWS])
        wsum = sb("wsum", [P, GP * PAIR])
        wsum_blk = sb("wsum_blk", [P, GP * PAIR, TU])
        wx = sb("wx", [P, 2 * D])
        rden = sb("rden", [P, 1])
        att, att_t = sb("att", [P, D]), sb("att_t", [P, D])
        user = sb("user", [P, D])
        bn = sb("bn", [P, 6])
        mv = sb("mv", [P, 2])
        vare, half, rstd = sb("vare", [P, 1]), sb("half", [P, 1]), sb("rstd", [P, 1])
        y0, y1 = sb("y0", [P, D]), sb("y1", [P, D])
        y = sb("y", [P, NGROUP, D])

        ps_sum = bank("ps_sum")
        ps_chain = bank("ps_chain")
        ps_max = bank("ps_max")
        ps_wx = bank("ps_wx")
        ps_group = bank("ps_group")
        ps_fin = bank("ps_fin")
        ps_prod = [bank("ps_prod0"), bank("ps_prod1")]
        c_mean = ps_chain[0:PUSERS, 0:D]
        c_spread = ps_chain[:, 256:512]
        c_query = ps_chain[:, 0:PAIR * D]

        x_loaded = [sem(f"x_loaded{i}") for i in range(SLOTS)]
        ld_weights, ld_mask_s, ld_mask_p = sem("ld_weights"), sem("ld_mask_s"), sem("ld_mask_p")
        ld_age_p, ld_users, ld_small = sem("ld_age_p"), sem("ld_users"), sem("ld_small")
        pool_setup, dve_setup, act_setup = sem("pool_setup"), sem("dve_setup"), sem("act_setup")
        wqk_done, wqk_ready = sem("wqk_done"), sem("wqk_ready")
        sp_exp_in, sp_exp, sp_ln_in, sp_ln, alpha_ready, decay_exp = (
            sem("sp_exp_in"), sem("sp_exp"), sem("sp_ln_in"), sem("sp_ln"), sem("alpha_ready"), sem("decay_exp"))
        gate_in, gate_exp, rows_ready, gathered = sem("gate_in"), sem("gate_exp"), sem("rows_ready"), sem("gathered")
        mask_ready = sem("mask_ready")
        mblk_ready = sem("mblk_ready")
        sum_done, sum_copied = sem("sum_done"), sem("sum_copied")
        mean_done, mean_ready = sem("mean_done"), sem("mean_ready")
        spread_done, spread_copied = sem("spread_done"), sem("spread_copied")
        query_done, query_ready = sem("query_done"), sem("query_ready")
        vprod_ready, gprod_ready = sem("vprod_ready"), sem("gprod_ready")
        dots_done, acts_done = sem("dots_done"), sem("acts_done")
        kept_ready, pmax_ready, pmax_turned = sem("kept_ready"), sem("pmax_ready"), sem("pmax_turned")
        umax_ready, nmax_ready, nmax_turned = sem("umax_ready"), sem("nmax_ready"), sem("nmax_turned")
        nmax_copied = sem("nmax_copied")
        exp_done, wts_ready, pblk_ready = sem("exp_done"), sem("wts_ready"), sem("pblk_ready")
        wx_done, wx_copied, wx_folded = sem("wx_done"), sem("wx_copied"), sem("wx_folded")
        wsum_ready, den_done, rden_ready, att_ready = (
            sem("wsum_ready"), sem("den_done"), sem("rden_ready"), sem("att_ready"))
        att_turned, att_t_ready, long_done = sem("att_turned"), sem("att_t_ready"), sem("long_done")
        user_ready, bn_ready, mv_ready, var_ready = sem("user_ready"), sem("bn_ready"), sem("mv_ready"), sem("var_ready")
        rstd_ready, norm_ready, scaled_ready, y_ready = (
            sem("rstd_ready"), sem("norm_ready"), sem("scaled_ready"), sem("y_ready"))
        pe_passed, dve_passed = sem("pe_passed"), sem("dve_passed")
        y_stored = sem("y_stored")

        block = ctx.enter_context(nc.Block())

        def steps(eng, step, last_step, first=0):
            for k in range(first, GP):
                step(0, k)
            with eng.Fori(1, NGROUP) as g:
                for k in range(GP):
                    step(g, k)
            for s in range(NPAIR, last_step + 1):
                step(s // GP, s % GP)

        def has(s, back, n=NPAIR):
            return not isinstance(s, int) or 0 <= s - back < n

        def rows(i, a, b):
            return x[:, i, a * D:b * D].rearrange("p (r d) -> p r d", d=D)

        @block.sync
        def _(sp):
            def store(q):
                sp.wait_ge(y_ready, q + 1)
                sp.dma_start(out[bass.ds(q * P, P), :], y[:, bass.ds(q, 1), :].rearrange("p q d -> p (q d)")
                             ).then_inc(y_stored, 16)

            def step(g, k):
                s = g * GP + k
                if has(s, GP):
                    sp.wait_ge(wx_done, s - GP + 1)
                for t in range(PAIR):
                    i = k * PAIR + t
                    sp.dma_start(x[:, i, :], items_t[bass.ds(s * PAIR + t, 1), :, :].rearrange("g p n -> (g p) n")
                                 ).then_inc(x_loaded[i], 16)

            sp.dma_start(mask_s[:, :, :], mask_pairs).then_inc(ld_mask_s, 16)
            sp.dma_start(mask_p[:, :, :], mask_t).then_inc(ld_mask_p, 16)
            steps(sp, step, NPAIR - 1)
            for q in range(NGROUP):
                store(q)
            sp.wait_ge(y_stored, 16 * NGROUP)

        @block.gpsimd
        def _(pool):
            made = [0]

            def link(ins):
                made[0] += 1
                ins.then_inc(pool_setup, 1)
                pool.wait_ge(pool_setup, made[0])

            def select(ap, op, pattern, base, mult, fill):
                link(nc.gpsimd.affine_select(out=ap, in_=ap, compare_op=op, fill=fill, base=base,
                                             pattern=pattern, channel_multiplier=mult))

            def build_mblk(s, k):
                if has(s, 2):
                    pool.wait_ge(sum_done, s - 1)
                for t in range(PAIR):
                    m = mask_f[:, bass.ds(s * PAIR + t, 1), :].rearrange("p g r -> p (g r)")
                    nc.gpsimd.tensor_tensor(mblk[:, k % 2, t, :, :], own[:, :].unsqueeze(1).broadcast_to([P, ROWS, TU]),
                                            m.unsqueeze(2).broadcast_to([P, ROWS, TU]), ALU.mult).then_inc(mblk_ready, 1)

            def build_pblk(s, k):
                pool.wait_ge(wts_ready, s * PAIR + PAIR)
                if has(s, 2):
                    pool.wait_ge(wx_done, s - 1)
                for t in range(PAIR):
                    nc.gpsimd.tensor_tensor(pblk[:, k % 2, t, :, :], own[:, :].unsqueeze(1).broadcast_to([P, ROWS, TU]),
                                            wts[:, t, :].unsqueeze(2).broadcast_to([P, ROWS, TU]), ALU.mult
                                            ).then_inc(pblk_ready, 1)

            def products(s, k, t):
                pool.wait_ge(query_ready, s + 1)
                if has(s, 1):
                    pool.wait_ge(acts_done, (s - 1) * PAIR + t + 1)
                r0 = DOTS + VPROD
                for a, b in GCHUNKS:
                    nc.gpsimd.tensor_tensor(gprod[:, t, a * D:b * D].rearrange("p (r d) -> p r d", d=D),
                                            rows((k % GP) * PAIR + t, r0 + a, r0 + b),
                                            query[:, k % 2, t, :].unsqueeze(1).broadcast_to([P, b - a, D]),
                                            ALU.mult).then_inc(gprod_ready, 1)

            def inverse_deviation(q):
                pool.wait_ge(var_ready, q + 1)
                nc.gpsimd.tensor_tensor(rstd[:, :], vare[:, :], half[:, :], ALU.pow).then_inc(rstd_ready, 1)

            link(nc.gpsimd.memset(own[:, :], 1.0))
            select(own[:, :], ALU.is_ge, [[-PU, TU]], 0, 1, 0.0)
            select(own[:, :], ALU.is_ge, [[PU, TU]], PU - 1, -1, 0.0)
            link(nc.gpsimd.memset(ident[:, :], 0.0))
            select(ident[:, :], ALU.not_equal, [[-1, P]], 0, 1, 1.0)
            pool.wait_ge(mask_ready, 1)
            build_mblk(0, 0)
            link(nc.gpsimd.memset(fold[:, :, :, :].rearrange("p a t u -> p (a t u)"), 0.0))
            for rr in range(2):
                for h in range(2):
                    select(fold[:, rr, :, :], ALU.not_equal, [[-64, PAIR], [-1, TU]], -(32 * h + TU * rr), 1, 1.0)
            link(nc.gpsimd.memset(spread[:, :], 1.0))
            select(spread[:, :], ALU.is_ge, [[1, PAIR * P]], 0, -PU, 0.0)
            select(spread[:, :], ALU.is_ge, [[-1, PAIR * P]], PU - 1, PU, 0.0)
            link(nc.gpsimd.iota(pos[:, :], [[1, NITEM]], base=0, channel_multiplier=0,
                                allow_small_or_imprecise_dtypes=True))
            link(nc.gpsimd.iota(user0[:, :], [[NITEM * P, NGROUP]], base=0, channel_multiplier=NITEM,
                                allow_small_or_imprecise_dtypes=True))
            link(nc.gpsimd.memset(ones[:, :], 1.0))
            link(nc.gpsimd.memset(half[:, :], -0.5))
            pool.wait_ge(rows_ready, 1)
            for q in range(NGROUP):
                for i in range(LAST):
                    nc.gpsimd.indirect_dma_start(
                        out=taken[:, q, i, :], out_offset=None, in_=items_rows,
                        in_offset=bass.IndirectOffsetOnAxis(ap=first_row[:, q:q + 1], axis=0),
                        element_offset=i * D).then_inc(gathered, 16)

            def step(g, k):
                s = g * GP + k
                if has(s, 0) and has(s, 1):
                    build_mblk(s, k)
                if has(s, 1):
                    products(s - 1, k - 1, 0)
                if has(s, 2):
                    build_pblk(s - 2, k)
                if has(s, 1):
                    products(s - 1, k - 1, 1)
                if k == 3 and has(g, 1, NGROUP):
                    inverse_deviation(g - 1)

            steps(pool, step, NPAIR + 3)
            assert made[0] == POOL_CONSTANTS

        @block.tensor
        def _(pe):
            def sum_rows(bank_, blk, i0, k, ms):
                for m0 in ms:
                    for t in range(PAIR):
                        for m in (m0, m0 + 1):
                            if m >= NPROD:
                                continue
                            n = min(2, ROWS - 2 * m)
                            c = 32 * (2 * t + m % 2)
                            w = blk[:, k % 2, t, 2 * m:2 * m + n, :].rearrange("p r u -> p (r u)")
                            ins = nc.tensor.matmul(bank_[c:c + n * TU, 0:n * D], w,
                                                   x[:, i0 + t, 2 * m * D:(2 * m + n) * D],
                                                   start=(m < 2), stop=(m >= NPROD - 2))
                return ins

            def fold_rows(dst, src):
                for rr in range(2):
                    ins = nc.tensor.matmul(dst, fold[:, rr, :, :].rearrange("p t u -> p (t u)"),
                                           src[:, rr * D:(rr + 1) * D], start=(rr == 0), stop=(rr == 1))
                return ins

            M0 = list(range(0, NPROD, 2))

            def step(g, k):
                s = g * GP + k
                i_new, i_old = k * PAIR, ((k - 2) % GP) * PAIR
                if has(s, 2):
                    pe.wait_ge(pmax_ready, s - 1)
                    if has(s, 3):
                        pe.wait_ge(exp_done, s - 2)
                    nc.tensor.transpose(ps_max[0:PAIR, 0:P], pmax[:, :], ident[:, :]).then_inc(pmax_turned, 1)
                if has(s, 0):
                    for t in range(PAIR):
                        pe.wait_ge(x_loaded[i_new + t], g * 16 + 16)
                    pe.wait_ge(mblk_ready, s * PAIR + PAIR)
                    if has(s, 1):
                        pe.wait_ge(sum_copied, s)
                    sum_rows(ps_sum, mblk, i_new, k, M0[:3])
                if has(s, 3):
                    pe.wait_ge(wx_copied, s - 2)
                    if k == 3 and has(g, 1):
                        pe.wait_ge(att_ready, g)
                    c = 32 * ((k - 3) % GP)
                    fold_rows(ps_group[c:c + PUSERS, 0:D], wx).then_inc(wx_folded, 1)
                if k == 2 and has(g, 1, NGROUP):
                    pe.wait_ge(wsum_ready, g)
                    nc.tensor.matmul(ps_fin[:, 0:1], wsum_blk[:, :, :].rearrange("p t u -> p (t u)"), ones[:, :],
                                     start=True, stop=True).then_inc(den_done, 1)
                if has(s, 2):
                    pe.wait_ge(nmax_ready, s - 1)
                    pe.sem_inc(pe_passed, 1)
                    nc.tensor.transpose(ps_max[:, P:P + PAIR], nmax[:, :], ident[0:PAIR, 0:PAIR]).then_inc(nmax_turned, 1)
                if has(s, 0):
                    sum_rows(ps_sum, mblk, i_new, k, M0[3:]).then_inc(sum_done, 1)
                if k == 3 and has(g, 1, NGROUP):
                    pe.wait_ge(att_ready, g)
                    nc.tensor.transpose(ps_fin[:, 128:256], att[:, :], ident[:, :]).then_inc(att_turned, 1)
                if has(s, 2):
                    pe.wait_ge(pblk_ready, (s - 2) * PAIR + PAIR)
                    if has(s, 3):
                        pe.wait_ge(wx_copied, s - 2)
                    sum_rows(ps_wx, pblk, i_old, k, M0[:2])
                if has(s, 0):
                    pe.wait_ge(sum_copied, s + 1)
                    if has(s, 1):
                        pe.wait_ge(query_ready, s)
                    fold_rows(c_mean, sums).then_inc(mean_done, 1)
                if has(s, 2):
                    sum_rows(ps_wx, pblk, i_old, k, M0[2:4])
                if has(s, 0):
                    pe.wait_ge(mean_ready, s + 1)
                    nc.tensor.matmul(c_spread, mean[:, :], spread[:, :], start=True, stop=True).then_inc(spread_done, 1)
                if has(s, 2):
                    sum_rows(ps_wx, pblk, i_old, k, M0[4:]).then_inc(wx_done, 1)
                if has(s, 0):
                    pe.wait_ge(spread_copied, s + 1)
                    for t in range(PAIR):
                        ins = nc.tensor.matmul(c_query[:, t * D:(t + 1) * D], mean_p[:, t * P:(t + 1) * P], wqk[:, :],
                                               start=True, stop=True)
                    ins.then_inc(query_done, 1)
                if k == 3 and has(g, 1, NGROUP):
                    pe.wait_ge(att_t_ready, g)
                    nc.tensor.matmul(ps_fin[:, 256:384], att_t[:, :], wv_t[:, :], start=True, stop=True
                                     ).then_inc(long_done, 1)

            pe.wait_ge(ld_weights, 48)
            pe.wait_ge(pool_setup, POOL_IDENT)
            nc.tensor.matmul(ps_fin[:, 0:D], wq[:, :], wk[:, :], start=True, stop=True)
            nc.tensor.transpose(ps_fin[:, 128:256], wv[:, :], ident[:, :]).then_inc(wqk_done, 1)
            pe.wait_ge(pool_setup, POOL_CONSTANTS)
            pe.wait_ge(wqk_ready, 2)
            steps(pe, step, NPAIR + 3)

        @block.scalar
        def _(act):
            def sum_products(s, k, t, part):
                def add(src, r):
                    return nc.scalar.activation(junk_a[:, t, r - DOTS, :], src, ACT.Copy, accum_out=score[:, k % 2, t, r:r + 1])
                if part == 0:
                    act.wait_ge(vprod_ready, s * PAIR + t + 1)
                    if has(s, 1):
                        act.wait_ge(kept_ready, s)
                    for r in range(VPROD):
                        add(ps_prod[t][:, r * D:(r + 1) * D], DOTS + r)
                else:
                    a, b = GCHUNKS[part - 1]
                    act.wait_ge(gprod_ready, (s * PAIR + t) * len(GCHUNKS) + part)
                    for r in range(a, b):
                        ins = add(gprod[:, t, r * D:(r + 1) * D], DOTS + VPROD + r)
                    if part == len(GCHUNKS):
                        ins.then_inc(acts_done, 1)

            def step(g, k):
                s = g * GP + k
                if has(s, 1):
                    sum_products(s - 1, k - 1, 0, 0)
                if has(s, 2):
                    act.wait_ge(nmax_turned, s - 1)
                    nc.scalar.activation(nmax_p[:, :], ps_max[:, P:P + PAIR], ACT.Copy).then_inc(nmax_copied, 1)
                    act.wait_ge(nmax_copied, s - 1)
                    for t in range(PAIR):
                        ins = nc.scalar.activation(ex[:, t, :], kept[:, t * ROWS:(t + 1) * ROWS], ACT.Exp,
                                                   bias=nmax_p[:, t:t + 1])
                    ins.then_inc(exp_done, 1)
                if has(s, 1):
                    sum_products(s - 1, k - 1, 0, 1)
                if has(s, 0):
                    act.wait_ge(sum_done, s + 1)
                    if has(s, 1):
                        act.wait_ge(mean_done, s)
                    nc.scalar.activation(sums[:, :], ps_sum[:, 0:2 * D], ACT.Copy).then_inc(sum_copied, 1)
                if has(s, 1):
                    sum_products(s - 1, k - 1, 0, 2)
                    sum_products(s - 1, k - 1, 1, 0)
                if has(s, 0):
                    act.wait_ge(spread_done, s + 1)
                    nc.scalar.activation(mean_p[:, :], c_spread, ACT.Copy).then_inc(spread_copied, 1)
                if has(s, 1):
                    sum_products(s - 1, k - 1, 1, 1)
                if has(s, 2):
                    act.wait_ge(wx_done, s - 1)
                    if has(s, 3):
                        act.wait_ge(wx_folded, s - 2)
                    nc.scalar.activation(wx[:, :], ps_wx[:, 0:2 * D], ACT.Copy).then_inc(wx_copied, 1)
                if has(s, 0):
                    act.wait_ge(query_done, s + 1)
                    if has(s, 2):
                        act.wait_ge(dots_done, (s - 1) * PAIR)
                        act.wait_ge(gprod_ready, (s - 1) * PAIR * len(GCHUNKS))
                    nc.scalar.activation(query[:, k % 2, :, :].rearrange("p t d -> p (t d)"), c_query, ACT.Copy
                                         ).then_inc(query_ready, 1)
                if has(s, 1):
                    sum_products(s - 1, k - 1, 1, 2)

            for dst, src in ((wq, Wq), (wk, Wk), (wv, Wv)):
                act.dma_start(dst[:, :], src).then_inc(ld_weights, 16)
            act.dma_start(mask_u[:, :, :], mask_n).then_inc(ld_users, 16)
            for dst, src in ((gam, gamma), (bet, beta), (gb, gate_b), (da, decay_alpha)):
                act.dma_start(dst[:, :], src.unsqueeze(0).broadcast_to([P, src.shape[0]])).then_inc(ld_small, 16)
            act.dma_start(gw[:, :], gate_w.broadcast_to([P, 2])).then_inc(ld_small, 16)
            act.dma_start(pop_u[:, :, :], pop_n).then_inc(ld_users, 16)
            act.dma_start(age_u[:, :, :], age_n).then_inc(ld_users, 16)
            act.dma_start(age_p[:, :].rearrange("p (g r) -> p g r", r=ROWS), age_t).then_inc(ld_age_p, 16)
            act.wait_ge(sp_exp_in, 1)
            nc.scalar.activation(soft[:, 1:2], soft[:, 0:1], ACT.Exp).then_inc(sp_exp, 1)
            act.wait_ge(sp_ln_in, 1)
            nc.scalar.activation(soft[:, 3:4], soft[:, 2:3], ACT.Ln).then_inc(sp_ln, 1)
            act.wait_ge(alpha_ready, 1)
            act.wait_ge(ld_age_p, 16)
            nc.scalar.activation(decay[:, :], age_p[:, :], ACT.Exp, scale=soft[:, 5:6]).then_inc(decay_exp, 1)
            step(0, 0)
            act.wait_ge(gate_in, 1)
            nc.scalar.activation(st[:, 12:14, :], st[:, 10:12, :], ACT.Exp).then_inc(gate_exp, 1)
            steps(act, step, NPAIR + 1, first=1)

        @block.vector
        def _(dve):
            made = [0]

            def link(ins):
                made[0] += 1
                ins.then_inc(dve_setup, 1)
                dve.wait_ge(dve_setup, made[0])

            V = nc.vector
            CNT, LOW, FIRST, DEN, RDEN, SPOP, SAGE, T0, T1, Z, ZNEG, ZABS, EZNEG, EZABS, GATE, GDIV = (
                st[:, n, :] for n in range(16))

            def setup_early():
                dve.wait_ge(ld_mask_p, 16)
                V.tensor_copy(mask_f[:, :, :], mask_p[:, :, :]).then_inc(mask_ready, 1)
                dve.wait_ge(ld_mask_s, 16)
                link(V.tensor_reduce(rcnt[:, :], mask_s[:, :, :], AX.X, ALU.add))
                link(V.tensor_scalar(rcnt[:, :], rcnt[:, :], 1e-6, None, ALU.add))
                link(V.reciprocal(rcnt[:, :], rcnt[:, :]))
                dve.wait_ge(ld_users, 48)
                link(V.tensor_reduce(CNT, mask_u[:, :, :], AX.X, ALU.add))
                link(V.tensor_scalar(CNT, CNT, 1.0, None, ALU.max))
                link(V.tensor_scalar(LOW, CNT, -float(LAST), None, ALU.add))
                link(V.tensor_scalar(FIRST, LOW, 0.0, None, ALU.max))
                dve.wait_ge(pool_setup, POOL_CONSTANTS)
                V.tensor_tensor(first_row[:, :], FIRST, user0[:, :], ALU.add).then_inc(rows_ready, 1)
                dve.wait_ge(wqk_done, 1)
                V.tensor_scalar(wqk[:, :], ps_fin[:, 0:D], SCALE, None, ALU.mult).then_inc(wqk_ready, 1)
                V.tensor_copy(wv_t[:, :], ps_fin[:, 128:256]).then_inc(wqk_ready, 1)

            def setup_decay():
                dve.wait_ge(ld_small, 80)
                V.scalar_tensor_tensor(out=soft[:, 0:1], in0=da[:, :], scalar=-1.0, in1=da[:, :],
                                       op0=ALU.mult, op1=ALU.min).then_inc(sp_exp_in, 1)
                dve.wait_ge(sp_exp, 1)
                V.tensor_scalar(soft[:, 2:3], soft[:, 1:2], 1.0, None, ALU.add).then_inc(sp_ln_in, 1)
                dve.wait_ge(sp_ln, 1)
                link(V.scalar_tensor_tensor(out=soft[:, 4:5], in0=da[:, :], scalar=0.0, in1=soft[:, 3:4],
                                            op0=ALU.max, op1=ALU.add))
                V.tensor_scalar(soft[:, 5:6], soft[:, 4:5], 1e-6, -1.0, ALU.add, ALU.mult).then_inc(alpha_ready, 1)
                dve.wait_ge(mask_ready, 1)
                mp = mask_f[:, :, :].rearrange("p g r -> p (g r)")
                link(V.tensor_scalar(hide[:, :], mp, -1.0, BIG, ALU.add, ALU.mult))
                dve.wait_ge(decay_exp, 1)
                link(V.scalar_tensor_tensor(out=decay[:, :], in0=decay[:, :], scalar=1e-12, in1=mp,
                                            op0=ALU.add, op1=ALU.mult))

            def setup_gate():
                link(V.tensor_scalar(DEN, CNT, float(LAST), None, ALU.min))
                link(V.reciprocal(RDEN, DEN))
                for q in range(NGROUP):
                    link(V.tensor_scalar(last[:, 0, :], pos[:, :], LOW[:, q:q + 1], None, ALU.is_ge))
                    link(V.scalar_tensor_tensor(out=last[:, 1, :], in0=pos[:, :], scalar=CNT[:, q:q + 1],
                                                in1=last[:, 0, :], op0=ALU.is_lt, op1=ALU.mult))
                    for src, total in ((pop_u, SPOP), (age_u, SAGE)):
                        link(V.scalar_tensor_tensor(out=junk_u[:, :], in0=src[:, q, :], scalar=1.0, in1=last[:, 1, :],
                                                    op0=ALU.mult, op1=ALU.mult, accum_out=total[:, q:q + 1]))
                link(V.tensor_scalar(T0, SPOP, gw[:, 0:1], None, ALU.mult))
                link(V.scalar_tensor_tensor(out=T1, in0=SAGE, scalar=gw[:, 1:2], in1=T0, op0=ALU.mult, op1=ALU.add))
                link(V.tensor_tensor(T0, T1, RDEN, ALU.mult))
                link(V.tensor_scalar(Z, T0, gb[:, 0:1], None, ALU.add))
                link(V.tensor_scalar(ZNEG, Z, 0.0, None, ALU.min))
                V.scalar_tensor_tensor(out=ZABS, in0=Z, scalar=-1.0, in1=Z, op0=ALU.mult, op1=ALU.min
                                       ).then_inc(gate_in, 1)
                dve.wait_ge(gate_exp, 1)
                link(V.tensor_scalar(T0, EZABS, 1.0, None, ALU.add))
                link(V.reciprocal(T1, T0))
                link(V.tensor_tensor(GATE, EZNEG, T1, ALU.mult))
                link(V.tensor_scalar(stay_[:, :], GATE, -1.0, 1.0, ALU.mult, ALU.add))
                link(V.tensor_tensor(GDIV, GATE, RDEN, ALU.mult))
                for i in range(LAST):
                    link(V.scalar_tensor_tensor(out=lw[:, i, :], in0=FIRST, scalar=float(i), in1=CNT,
                                                op0=ALU.add, op1=ALU.is_lt))
                    link(V.tensor_tensor(lw[:, i, :], lw[:, i, :], GDIV, ALU.mult))

            def setup_short():
                dve.wait_ge(gathered, 16 * NGROUP * LAST)
                for i in range(LAST):
                    for q in range(NGROUP):
                        w, src = lw[:, i, q:q + 1], taken[:, q, i, :]
                        ins = (V.tensor_scalar(short[:, q, :], src, w, None, ALU.mult) if i == 0 else
                               V.scalar_tensor_tensor(out=short[:, q, :], in0=src, scalar=w, in1=short[:, q, :],
                                                      op0=ALU.mult, op1=ALU.add))
                        if q == NGROUP - 1:
                            link(ins)

            def mask_and_max(s, k):
                dve.wait_ge(acts_done, s * PAIR + PAIR)
                dve.wait_ge(dots_done, s * PAIR + PAIR)
                V.tensor_tensor(kept[:, :], score[:, k % 2, :, :].rearrange("p t r -> p (t r)"),
                                hide[:, bass.ds(s * PROWS, PROWS)], ALU.add).then_inc(kept_ready, 1)
                dve.wait_ge(kept_ready, s + 1)
                V.tensor_reduce(pmax[:, :], kept[:, :].rearrange("p (t r) -> p t r", t=PAIR), AX.X, ALU.max
                                ).then_inc(pmax_ready, 1)

            def user_max(s):
                dve.wait_ge(pmax_turned, s + 1)
                V.tensor_reduce(umax[:, :], ps_max[0:PAIR, 0:P].rearrange("t (u c) -> t u c", c=PU), AX.X, ALU.max
                                ).then_inc(umax_ready, 1)
                dve.wait_ge(umax_ready, s + 1)
                V.tensor_scalar(nmax[:, :].rearrange("t (u c) -> t u c", c=PU),
                                umax[:, :].unsqueeze(2).broadcast_to([PAIR, TU, PU]), -1.0, None, ALU.mult
                                ).then_inc(nmax_ready, 1)

            def weights(s, k):
                dve.wait_ge(exp_done, s + 1)
                if has(s, 1):
                    dve.wait_ge(pblk_ready, s * PAIR)
                for t in range(PAIR):
                    i = (k % GP) * PAIR + t
                    V.scalar_tensor_tensor(out=wts[:, t, :], in0=ex[:, t, :], scalar=1.0,
                                           in1=decay[:, bass.ds(s * PROWS + t * ROWS, ROWS)],
                                           op0=ALU.mult, op1=ALU.mult, accum_out=wsum[:, i:i + 1]).then_inc(wts_ready, 1)

            def products(s, k, t):
                dve.wait_ge(query_ready, s + 1)
                if has(s, 1):
                    dve.wait_ge(acts_done, (s - 1) * PAIR + t + 1)
                V.tensor_tensor(ps_prod[t][:, 0:VPROD * D].rearrange("p (r d) -> p r d", d=D),
                                rows((k % GP) * PAIR + t, DOTS, DOTS + VPROD),
                                query[:, k % 2, t, :].unsqueeze(1).broadcast_to([P, VPROD, D]),
                                ALU.mult).then_inc(vprod_ready, 1)

            def dots(s, k, t, a, b):
                for r in range(a, b):
                    ins = V.scalar_tensor_tensor(out=junk_v[:, t, r, :], in0=x[:, (k % GP) * PAIR + t, r * D:(r + 1) * D],
                                                 scalar=1.0, in1=query[:, k % 2, t, :], op0=ALU.mult, op1=ALU.mult,
                                                 accum_out=score[:, k % 2, t, r:r + 1])
                if b == DOTS:
                    ins.then_inc(dots_done, 1)

            def finish_att(g):
                dve.wait_ge(den_done, g)
                V.reciprocal(rden[:, :], ps_fin[:, 0:1]).then_inc(rden_ready, 1)
                dve.wait_ge(rden_ready, g)
                dve.wait_ge(wx_folded, g * GP)
                V.tensor_scalar(att[:, :], ps_group[:, 0:D], rden[:, :], None, ALU.mult).then_inc(att_ready, 1)

            def finish_user(g):
                dve.wait_ge(long_done, g)
                q = g - 1
                V.scalar_tensor_tensor(out=user[:, :], in0=ps_fin[:, 256:384], scalar=stay_[:, bass.ds(q, 1)],
                                       in1=short[:, bass.ds(q, 1), :].rearrange("p q d -> p (q d)"),
                                       op0=ALU.mult, op1=ALU.add).then_inc(user_ready, 1)
                dve.wait_ge(user_ready, g)
                V.bn_stats(bn[:, :], user[:, :]).then_inc(bn_ready, 1)
                dve.wait_ge(bn_ready, g)
                dve.sem_inc(dve_passed, 1)
                V.bn_aggr(mv[:, :], bn[:, :]).then_inc(mv_ready, 1)
                dve.wait_ge(mv_ready, g)
                V.tensor_scalar(vare[:, :], mv[:, 1:2], 1e-5, None, ALU.add).then_inc(var_ready, 1)

            def finish_norm(g):
                dve.wait_ge(rstd_ready, g)
                q = g - 1
                V.tensor_scalar(y0[:, :], user[:, :], mv[:, 0:1], rstd[:, :], ALU.subtract, ALU.mult
                                ).then_inc(norm_ready, 1)
                dve.wait_ge(norm_ready, g)
                V.tensor_tensor(y1[:, :], y0[:, :], gam[:, :], ALU.mult).then_inc(scaled_ready, 1)
                dve.wait_ge(scaled_ready, g)
                V.tensor_tensor(y[:, bass.ds(q, 1), :].rearrange("p q d -> p (q d)"), y1[:, :], bet[:, :], ALU.add
                                ).then_inc(y_ready, 1)

            def step(g, k):
                s = g * GP + k
                fin = has(g, 1, NGROUP)
                if has(s, 2):
                    mask_and_max(s - 2, k)
                if has(s, 1):
                    products(s - 1, k - 1, 0)
                if has(s, 2):
                    user_max(s - 2)
                if has(s, 1):
                    dots(s - 1, k - 1, 0, 0, 4)
                if has(s, 2):
                    weights(s - 2, k - 2)
                if k == 1 and fin:
                    dve.wait_ge(wts_ready, (s - 1) * PAIR)
                    V.tensor_tensor(wsum_blk[:, :, :], own[:, :].unsqueeze(1).broadcast_to([P, GP * PAIR, TU]),
                                    wsum[:, :].unsqueeze(2).broadcast_to([P, GP * PAIR, TU]), ALU.mult
                                    ).then_inc(wsum_ready, 1)
                if has(s, 1):
                    dots(s - 1, k - 1, 0, 4, DOTS)
                    products(s - 1, k - 1, 1)
                if k == 2 and fin:
                    finish_att(g)
                if has(s, 0):
                    dve.wait_ge(mean_done, s + 1)
                    V.tensor_scalar(mean[:, :], c_mean, rcnt[:, bass.ds(s, 1)], None, ALU.mult).then_inc(mean_ready, 1)
                if has(s, 1):
                    dots(s - 1, k - 1, 1, 0, 6)
                if k == 3 and fin:
                    dve.wait_ge(att_turned, g)
                    V.tensor_copy(att_t[:, :], ps_fin[:, 128:256]).then_inc(att_t_ready, 1)
                if has(s, 1):
                    dots(s - 1, k - 1, 1, 6, DOTS)
                if k == 3 and fin:
                    finish_user(g)
                    finish_norm(g)

            setup_early()
            setup_decay()
            step(0, 0)
            setup_gate()
            setup_short()
            steps(dve, step, NPAIR + 3, first=1)

    return nc


def kernel(**inputs):
    import numpy as _np
    import concourse.bacc as _bacc
    from concourse.bass_utils import run_bass_kernel_spmd as _run

    names = ["r_hist_items", "r_hist_mask", "r_hist_age_hours", "r_hist_popularity", "L0_rec_Wq", "L0_rec_Wk",
             "L0_rec_Wv", "L0_rec_gate_w", "L0_rec_gate_b", "L0_rec_ln_gamma", "L0_rec_ln_beta", "L0_rec_decay_alpha"]
    nc = _bacc.Bacc("TRN2", target_bir_lowering=False, num_devices=1)
    arrays, args = {}, []
    for name in names:
        a = _np.ascontiguousarray(inputs[name])
        arrays[f"in_{name}_dram"] = a
        args.append(nc.dram_tensor(f"in_{name}_dram", a.shape, mybir.dt.from_np(a.dtype), kind="ExternalInput").ap())
    out = nc.dram_tensor("out_dram", (NUSER, D), F32, kind="ExternalOutput").ap()
    build(nc, *args, out)
    r = _run(nc, [arrays], core_ids=[0])
    return r.results[0]["out_dram"]
```

```python
import concourse.bass as bass
from concourse import mybir
from concourse.alu_op_type import AluOpType as ALU
from contextlib import ExitStack

F32 = mybir.dt.float32
U8 = mybir.dt.uint8
I32 = mybir.dt.int32
U32 = mybir.dt.uint32
ACT = mybir.ActivationFunctionType
AX = mybir.AxisListType

NUSER, NITEM, D = 512, 200, 128
P = 128
LAST = 5
PU = 8
ROWS = NITEM // PU
TU = P // PU
NTILE = NUSER // TU
PAIR = 2
NPAIR = NTILE // PAIR
GP = 4
NGROUP = NPAIR // GP
SLOTS = GP * PAIR
PROWS = PAIR * ROWS
PUSERS = PAIR * TU
NPROD = (ROWS + 1) // 2
BIG = 3.0e38
SCALE = float(D) ** -0.5

DOTS = 14
VPROD = 4
GPROD = ROWS - DOTS - VPROD
GCHUNKS = ((0, GPROD // 2), (GPROD // 2, GPROD))
POOL_IDENT = 5
POOL_CONSTANTS = 21


def build(nc, items, mask, age, pop, Wq, Wk, Wv, gate_w, gate_b, gamma, beta, decay_alpha, out):
    items_t = items.rearrange("u t d -> (u t d)").rearrange("(g p n) -> g p n", p=P, n=ROWS * D)
    items_rows = items.rearrange("u t d -> (u t) d")
    mask_t = mask.rearrange("u t -> (u t)").rearrange("(g p r) -> p g r", p=P, r=ROWS)
    age_t = age.rearrange("u t -> (u t)").rearrange("(g p r) -> p g r", p=P, r=ROWS)
    mask_pairs = mask.rearrange("(s u) t -> u s t", u=PUSERS)
    mask_n, age_n, pop_n = (a.rearrange("(q u) t -> u q t", u=P) for a in (mask, age, pop))

    ctx = ExitStack()
    with ctx:
        def sb(name, shape, dt=F32):
            return ctx.enter_context(nc.sbuf_tensor(name, shape, dt))

        def bank(name):
            return ctx.enter_context(nc.psum_tensor(name, [P, 512], F32))

        def sem(name):
            return ctx.enter_context(nc.semaphore(name))

        x = sb("x", [P, SLOTS, ROWS * D])
        wq, wk, wv = sb("wq", [P, D]), sb("wk", [P, D]), sb("wv", [P, D])
        wqk, wv_t = sb("wqk", [P, D]), sb("wv_t", [P, D])
        ident = sb("ident", [P, P])
        ones = sb("ones", [P, 1])
        own = sb("own", [P, TU])
        fold = sb("fold", [P, 2, PAIR, TU])
        unfold = sb("unfold", [PUSERS, PAIR, 2, 2, TU])
        spread = sb("spread", [P, 2, PAIR, TU, PU])
        gam, bet = sb("gam", [P, D]), sb("bet", [P, D])
        gw, gb, da = sb("gw", [P, 2]), sb("gb", [P, 1]), sb("da", [P, 1])
        mask_p = sb("mask_p", [P, NTILE, ROWS], U8)
        mask_f = sb("mask_f", [P, NTILE, ROWS])
        mask_s = sb("mask_s", [PUSERS, NPAIR, NITEM], U8)
        mask_u = sb("mask_u", [P, NGROUP, NITEM], U8)
        age_p = sb("age_p", [P, NTILE * ROWS])
        decay = sb("decay", [P, NTILE * ROWS])
        hide = sb("hide", [P, NTILE * ROWS])
        age_u, pop_u = sb("age_u", [P, NGROUP, NITEM]), sb("pop_u", [P, NGROUP, NITEM])
        pos = sb("pos", [P, NITEM])
        rcnt = sb("rcnt", [PUSERS, NPAIR])
        st = sb("st", [P, 16, NGROUP])
        soft = sb("soft", [P, 8])
        stay_ = sb("stay", [P, NGROUP])
        last = sb("last", [P, 2, NITEM])
        junk_u = sb("junk_u", [P, NITEM])
        junk_v = sb("junk_v", [P, PAIR, DOTS, D])
        first_row = sb("first_row", [P, NGROUP], U32)
        user0 = sb("user0", [P, NGROUP])
        group_row = sb("group_row", [P, 1], U32)
        taken = sb("taken", [P, LAST, D])
        lw = sb("lw", [P, LAST, NGROUP])
        short = sb("short", [P, D])
        mblk = sb("mblk", [P, 2, PAIR, ROWS, TU])
        pblk = sb("pblk", [P, 2, PAIR, ROWS, TU])
        sums = sb("sums", [P, 2 * D])
        rcnt_rows = sb("rcnt_rows", [P, NPAIR])
        mean_p = sb("mean_p", [P, PAIR * P])
        query = sb("query", [P, 2, PAIR, D])
        vprod = sb("vprod", [P, PAIR, VPROD * D])
        gprod = sb("gprod", [P, PAIR, GPROD * D])
        score = sb("score", [P, 2, PAIR, ROWS])
        kept = sb("kept", [P, PROWS])
        pmax = sb("pmax", [P, PAIR])
        umax = sb("umax", [PAIR, TU])
        nmax = sb("nmax", [PAIR, P])
        nmax_p = sb("nmax_p", [P, PAIR])
        ex = sb("ex", [P, PAIR, ROWS])
        wts = sb("wts", [P, PAIR, ROWS])
        wsum = sb("wsum", [P, GP * PAIR])
        wsum_blk = sb("wsum_blk", [P, GP * PAIR, TU])
        wx = sb("wx", [P, 2 * D])
        rden = sb("rden", [P, 1])
        att, att_t = sb("att", [P, D]), sb("att_t", [P, D])
        user = sb("user", [P, D])
        bn = sb("bn", [P, 6])
        mv = sb("mv", [P, 2])
        vare, half, rstd = sb("vare", [P, 1]), sb("half", [P, 1]), sb("rstd", [P, 1])
        y0, y1 = sb("y0", [P, D]), sb("y1", [P, D])
        y = sb("y", [P, NGROUP, D])

        ps_sum = bank("ps_sum")
        ps_chain = bank("ps_chain")
        ps_max = bank("ps_max")
        ps_wx = bank("ps_wx")
        ps_group = bank("ps_group")
        ps_fin = bank("ps_fin")
        c_mean = ps_chain[:, 256:512]
        c_query = ps_chain[:, 0:PAIR * D]

        x_loaded = [sem(f"x_loaded{i}") for i in range(SLOTS)]
        ld_weights, ld_mask_s, ld_mask_p = sem("ld_weights"), sem("ld_mask_s"), sem("ld_mask_p")
        ld_mask_u, ld_age_p, ld_users, ld_small = sem("ld_mask_u"), sem("ld_age_p"), sem("ld_users"), sem("ld_small")
        pool_setup, dve_setup, act_setup = sem("pool_setup"), sem("dve_setup"), sem("act_setup")
        wqk_done, wqk_ready = sem("wqk_done"), sem("wqk_ready")
        sp_exp_in, sp_exp, sp_ln_in, sp_ln, alpha_ready, decay_exp = (
            sem("sp_exp_in"), sem("sp_exp"), sem("sp_ln_in"), sem("sp_ln"), sem("alpha_ready"), sem("decay_exp"))
        gate_in, gate_exp, rows_ready = sem("gate_in"), sem("gate_exp"), sem("rows_ready")
        short_part = sem("short_part")
        row_copied, gathered = sem("row_copied"), sem("gathered")
        mask_ready = sem("mask_ready")
        mblk_ready = sem("mblk_ready")
        sum_done, sum_copied = sem("sum_done"), sem("sum_copied")
        rcnt_ready, rcnt_spread, rcnt_rows_ready = sem("rcnt_ready"), sem("rcnt_spread"), sem("rcnt_rows_ready")
        mean_done, mean_copied = sem("mean_done"), sem("mean_copied")
        query_done, query_ready = sem("query_done"), sem("query_ready")
        vprod_ready, gprod_ready = sem("vprod_ready"), sem("gprod_ready")
        dots_done, vsums_done, gsums_done = sem("dots_done"), sem("vsums_done"), sem("gsums_done")
        kept_ready, pmax_ready, pmax_turned = sem("kept_ready"), sem("pmax_ready"), sem("pmax_turned")
        umax_ready, nmax_ready, nmax_turned = sem("umax_ready"), sem("nmax_ready"), sem("nmax_turned")
        nmax_copied = sem("nmax_copied")
        exp_done, wts_ready, pblk_ready = sem("exp_done"), sem("wts_ready"), sem("pblk_ready")
        wx_done, wx_copied, wx_folded = sem("wx_done"), sem("wx_copied"), sem("wx_folded")
        wsum_ready, den_done, rden_ready, att_ready = (
            sem("wsum_ready"), sem("den_done"), sem("rden_ready"), sem("att_ready"))
        att_turned, att_t_ready, long_done = sem("att_turned"), sem("att_t_ready"), sem("long_done")
        user_ready, bn_ready, mv_ready, var_ready = sem("user_ready"), sem("bn_ready"), sem("mv_ready"), sem("var_ready")
        rstd_ready, norm_ready, scaled_ready, y_ready = (
            sem("rstd_ready"), sem("norm_ready"), sem("scaled_ready"), sem("y_ready"))
        pe_passed, pool_passed, dve_passed = sem("pe_passed"), sem("pool_passed"), sem("dve_passed")
        y_stored = sem("y_stored")

        block = ctx.enter_context(nc.Block())

        def steps(eng, step, last_step, first=0):
            for k in range(first, GP):
                step(0, k)
            with eng.Fori(1, NGROUP) as g:
                for k in range(GP):
                    step(g, k)
            for s in range(NPAIR, last_step + 1):
                step(s // GP, s % GP)

        def has(s, back, n=NPAIR):
            return not isinstance(s, int) or 0 <= s - back < n

        def rows(i, a, b):
            return x[:, i, a * D:b * D].rearrange("p (r d) -> p r d", d=D)

        @block.sync
        def _(sp):
            def store(q):
                sp.wait_ge(y_ready, q + 1)
                sp.dma_start(out[bass.ds(q * P, P), :], y[:, bass.ds(q, 1), :].rearrange("p q d -> p (q d)")
                             ).then_inc(y_stored, 16)

            def step(g, k):
                s = g * GP + k
                if has(s, GP):
                    sp.wait_ge(wx_done, s - GP + 1)
                for t in range(PAIR):
                    i = k * PAIR + t
                    sp.dma_start(x[:, i, :], items_t[bass.ds(s * PAIR + t, 1), :, :].rearrange("g p n -> (g p) n")
                                 ).then_inc(x_loaded[i], 16)

            sp.dma_start(mask_p[:, :, :], mask_t).then_inc(ld_mask_p, 16)
            sp.dma_start(mask_s[:, :, :], mask_pairs).then_inc(ld_mask_s, 16)
            for dst, src in ((wq, Wq), (wk, Wk), (wv, Wv)):
                sp.dma_start(dst[:, :], src).then_inc(ld_weights, 16)
            sp.dma_start(mask_u[:, :, :], mask_n).then_inc(ld_mask_u, 16)
            sp.dma_start(gw[:, :], gate_w.broadcast_to([P, 2])).then_inc(ld_small, 16)
            for dst, src in ((da, decay_alpha), (gb, gate_b), (gam, gamma), (bet, beta)):
                sp.dma_start(dst[:, :], src.unsqueeze(0).broadcast_to([P, src.shape[0]])).then_inc(ld_small, 16)
            sp.dma_start(pop_u[:, :, :], pop_n).then_inc(ld_users, 16)
            sp.dma_start(age_u[:, :, :], age_n).then_inc(ld_users, 16)
            step(0, 0)
            sp.dma_start(age_p[:, :].rearrange("p (g r) -> p g r", r=ROWS), age_t).then_inc(ld_age_p, 16)
            steps(sp, step, NPAIR - 1, first=1)
            for q in range(NGROUP):
                store(q)
            sp.wait_ge(y_stored, 16 * NGROUP)

        @block.gpsimd
        def _(pool):
            made = [0]

            def link(ins):
                made[0] += 1
                ins.then_inc(pool_setup, 1)
                pool.wait_ge(pool_setup, made[0])

            def select(ap, op, pattern, base, mult, fill):
                link(nc.gpsimd.affine_select(out=ap, in_=ap, compare_op=op, fill=fill, base=base,
                                             pattern=pattern, channel_multiplier=mult))

            def build_mblk(s, k):
                if has(s, 2):
                    pool.wait_ge(sum_done, s - 1)
                for t in range(PAIR):
                    m = mask_f[:, bass.ds(s * PAIR + t, 1), :].rearrange("p g r -> p (g r)")
                    nc.gpsimd.tensor_tensor(mblk[:, k % 2, t, :, :], own[:, :].unsqueeze(1).broadcast_to([P, ROWS, TU]),
                                            m.unsqueeze(2).broadcast_to([P, ROWS, TU]), ALU.mult).then_inc(mblk_ready, 1)

            def build_pblk(s, k):
                pool.wait_ge(wts_ready, s * PAIR + PAIR)
                if has(s, 2):
                    pool.wait_ge(wx_done, s - 1)
                for t in range(PAIR):
                    nc.gpsimd.tensor_tensor(pblk[:, k % 2, t, :, :], own[:, :].unsqueeze(1).broadcast_to([P, ROWS, TU]),
                                            wts[:, t, :].unsqueeze(2).broadcast_to([P, ROWS, TU]), ALU.mult
                                            ).then_inc(pblk_ready, 1)

            def products(s, k, t):
                pool.wait_ge(query_ready, s + 1)
                if has(s, 1):
                    pool.wait_ge(gsums_done, (s - 1) * PAIR + t + 1)
                r0 = DOTS + VPROD
                for a, b in GCHUNKS:
                    nc.gpsimd.tensor_tensor(gprod[:, t, a * D:b * D].rearrange("p (r d) -> p r d", d=D),
                                            rows((k % GP) * PAIR + t, r0 + a, r0 + b),
                                            query[:, k % 2, t, :].unsqueeze(1).broadcast_to([P, b - a, D]),
                                            ALU.mult).then_inc(gprod_ready, 1)

            def inverse_deviation(q):
                pool.wait_ge(var_ready, q + 1)
                nc.gpsimd.tensor_tensor(rstd[:, :], vare[:, :], half[:, :], ALU.pow).then_inc(rstd_ready, 1)

            link(nc.gpsimd.memset(own[:, :], 1.0))
            select(own[:, :], ALU.is_ge, [[-PU, TU]], 0, 1, 0.0)
            select(own[:, :], ALU.is_ge, [[PU, TU]], PU - 1, -1, 0.0)
            link(nc.gpsimd.memset(ident[:, :], 0.0))
            select(ident[:, :], ALU.not_equal, [[-1, P]], 0, 1, 1.0)
            pool.wait_ge(mask_ready, 1)
            build_mblk(0, 0)
            link(nc.gpsimd.memset(fold[:, :, :, :].rearrange("p a t u -> p (a t u)"), 0.0))
            for rr in range(2):
                for h in range(2):
                    select(fold[:, rr, :, :], ALU.not_equal, [[-64, PAIR], [-1, TU]], -(32 * h + TU * rr), 1, 1.0)
            link(nc.gpsimd.memset(unfold[:, :, :, :, :].rearrange("q t h r u -> q (t h r u)"), 0.0))
            for h in range(2):
                for rr in range(2):
                    select(unfold[:, :, h, rr, :], ALU.not_equal, [[-TU, PAIR], [-1, TU]], 0, 1, 1.0)
            for rr in range(2):
                link(nc.gpsimd.tensor_copy(spread[:, rr, :, :, :].rearrange("p t u c -> p (t u) c"),
                                           fold[:, rr, :, :].rearrange("p t u -> p (t u)").unsqueeze(2)
                                           .broadcast_to([P, PUSERS, PU])))
            link(nc.gpsimd.iota(pos[:, :], [[1, NITEM]], base=0, channel_multiplier=0,
                                allow_small_or_imprecise_dtypes=True))
            link(nc.gpsimd.iota(user0[:, :], [[NITEM * P, NGROUP]], base=0, channel_multiplier=NITEM,
                                allow_small_or_imprecise_dtypes=True))
            link(nc.gpsimd.memset(ones[:, :], 1.0))
            link(nc.gpsimd.memset(half[:, :], -0.5))
            def gather(g, k):
                if k == 1:
                    if has(g, 1):
                        pool.wait_ge(short_part, g * LAST)
                    nc.gpsimd.tensor_copy(group_row[:, :], first_row[:, bass.ds(g, 1)]).then_inc(row_copied, 1)
                    pool.wait_ge(row_copied, g + 1)
                    pool.sem_inc(pool_passed, 1)
                for i in range(LAST)[2 * k - 2:2 * k]:
                    nc.gpsimd.indirect_dma_start(
                        out=taken[:, i, :], out_offset=None, in_=items_rows,
                        in_offset=bass.IndirectOffsetOnAxis(ap=group_row[:, :], axis=0),
                        element_offset=i * D).then_inc(gathered, 16)

            def step(g, k):
                s = g * GP + k
                if has(s, 0) and has(s, 1):
                    build_mblk(s, k)
                if k > 0 and has(s, 0):
                    gather(g, k)
                if has(s, 1):
                    for t in range(PAIR):
                        products(s - 1, k - 1, t)
                if has(s, 2):
                    build_pblk(s - 2, k)
                if k == 3 and has(g, 1, NGROUP):
                    inverse_deviation(g - 1)

            pool.wait_ge(rows_ready, 1)
            steps(pool, step, NPAIR + 3)
            assert made[0] == POOL_CONSTANTS

        @block.tensor
        def _(pe):
            def sum_rows(bank_, blk, i0, k, ms):
                for m0 in ms:
                    for t in range(PAIR):
                        for m in (m0, m0 + 1):
                            if m >= NPROD:
                                continue
                            n = min(2, ROWS - 2 * m)
                            c = 32 * (2 * t + m % 2)
                            w = blk[:, k % 2, t, 2 * m:2 * m + n, :].rearrange("p r u -> p (r u)")
                            ins = nc.tensor.matmul(bank_[c:c + n * TU, 0:n * D], w,
                                                   x[:, i0 + t, 2 * m * D:(2 * m + n) * D],
                                                   start=(m < 2), stop=(m >= NPROD - 2))
                return ins

            def mean_rows(src):
                for rr in range(2):
                    ins = nc.tensor.matmul(c_mean, src[:, rr * D:(rr + 1) * D],
                                           spread[:, rr, :, :, :].rearrange("p t u c -> p (t u c)"),
                                           start=(rr == 0), stop=(rr == 1))
                return ins

            def fold_rows(dst, src):
                for rr in range(2):
                    ins = nc.tensor.matmul(dst, fold[:, rr, :, :].rearrange("p t u -> p (t u)"),
                                           src[:, rr * D:(rr + 1) * D], start=(rr == 0), stop=(rr == 1))
                return ins

            M0 = list(range(0, NPROD, 2))

            def step(g, k):
                s = g * GP + k
                i_new, i_old = k * PAIR, ((k - 2) % GP) * PAIR
                if has(s, 0):
                    for t in range(PAIR):
                        pe.wait_ge(x_loaded[i_new + t], g * 16 + 16)
                    pe.wait_ge(mblk_ready, s * PAIR + PAIR)
                    if has(s, 1):
                        pe.wait_ge(sum_copied, s)
                    sum_rows(ps_sum, mblk, i_new, k, M0[:2])
                if has(s, 2):
                    pe.wait_ge(pmax_ready, s - 1)
                    if has(s, 3):
                        pe.wait_ge(exp_done, s - 2)
                    nc.tensor.transpose(ps_max[0:PAIR, 0:P], pmax[:, :], ident[:, :]).then_inc(pmax_turned, 1)
                if has(s, 0):
                    sum_rows(ps_sum, mblk, i_new, k, M0[2:4])
                if has(s, 2):
                    pe.wait_ge(nmax_ready, s - 1)
                    pe.sem_inc(pe_passed, 1)
                    nc.tensor.transpose(ps_max[:, P:P + PAIR], nmax[:, :], ident[0:PAIR, 0:PAIR]).then_inc(nmax_turned, 1)
                if k == 3 and has(g, 1, NGROUP):
                    pe.wait_ge(att_t_ready, g)
                    nc.tensor.matmul(ps_fin[:, 256:384], att_t[:, :], wv_t[:, :], start=True, stop=True
                                     ).then_inc(long_done, 1)
                if has(s, 0):
                    sum_rows(ps_sum, mblk, i_new, k, M0[4:]).then_inc(sum_done, 1)
                if has(s, 3):
                    pe.wait_ge(wx_copied, s - 2)
                    if k == 3 and has(g, 1):
                        pe.wait_ge(att_ready, g)
                    c = 32 * ((k - 3) % GP)
                    fold_rows(ps_group[c:c + PUSERS, 0:D], wx).then_inc(wx_folded, 1)
                if k == 2 and has(g, 1, NGROUP):
                    pe.wait_ge(wsum_ready, g)
                    nc.tensor.matmul(ps_fin[:, 0:1], wsum_blk[:, :, :].rearrange("p t u -> p (t u)"), ones[:, :],
                                     start=True, stop=True).then_inc(den_done, 1)
                if has(s, 0):
                    pe.wait_ge(sum_copied, s + 1)
                    if has(s, 1):
                        pe.wait_ge(query_ready, s)
                    mean_rows(sums).then_inc(mean_done, 1)
                if has(s, 2):
                    pe.wait_ge(pblk_ready, (s - 2) * PAIR + PAIR)
                    if has(s, 3):
                        pe.wait_ge(wx_copied, s - 2)
                    sum_rows(ps_wx, pblk, i_old, k, M0[:3])
                if has(s, 0):
                    pe.wait_ge(mean_copied, s + 1)
                    for t in range(PAIR):
                        ins = nc.tensor.matmul(c_query[:, t * D:(t + 1) * D], mean_p[:, t * P:(t + 1) * P], wqk[:, :],
                                               start=True, stop=True)
                    ins.then_inc(query_done, 1)
                if has(s, 2):
                    sum_rows(ps_wx, pblk, i_old, k, M0[3:]).then_inc(wx_done, 1)
                if k == 2 and has(g, 1, NGROUP):
                    pe.wait_ge(att_ready, g)
                    nc.tensor.transpose(ps_fin[:, 128:256], att[:, :], ident[:, :]).then_inc(att_turned, 1)

            pe.wait_ge(ld_weights, 48)
            pe.wait_ge(pool_setup, POOL_IDENT)
            nc.tensor.matmul(ps_fin[:, 0:D], wq[:, :], wk[:, :], start=True, stop=True)
            nc.tensor.transpose(ps_fin[:, 128:256], wv[:, :], ident[:, :]).then_inc(wqk_done, 1)
            pe.wait_ge(pool_setup, POOL_CONSTANTS)
            pe.wait_ge(wqk_ready, 2)
            pe.wait_ge(rcnt_ready, 1)
            nc.tensor.matmul(ps_fin[:, 0:NPAIR], unfold[:, :, :, :, :].rearrange("q t h r u -> q (t h r u)"), rcnt[:, :],
                             start=True, stop=True).then_inc(rcnt_spread, 1)
            steps(pe, step, NPAIR + 3)

        @block.scalar
        def _(act):
            def sum_products(s, k, t, which, a, b):
                prod, r0, n = (vprod, DOTS, VPROD) if which == "v" else (gprod, DOTS + VPROD, GPROD)
                if which == "v" and a == 0:
                    act.wait_ge(vprod_ready, s * PAIR + t + 1)
                    if has(s, 2):
                        act.wait_ge(kept_ready, s - 1)
                if which == "g":
                    act.wait_ge(gprod_ready, (s * PAIR + t) * len(GCHUNKS) + (1 if b <= GCHUNKS[0][1] else 2))
                for r in range(a, b):
                    src = prod[:, t, r * D:(r + 1) * D]
                    ins = nc.scalar.activation(src, src, ACT.Copy, accum_out=score[:, k % 2, t, r0 + r:r0 + r + 1])
                if b == n:
                    ins.then_inc(vsums_done if which == "v" else gsums_done, 1)

            def step(g, k):
                s = g * GP + k
                if has(s, 1):
                    sum_products(s - 1, k - 1, 0, "v", 0, VPROD)
                if has(s, 3):
                    act.wait_ge(wx_done, s - 2)
                    if has(s, 4):
                        act.wait_ge(wx_folded, s - 3)
                    nc.scalar.activation(wx[:, :], ps_wx[:, 0:2 * D], ACT.Copy).then_inc(wx_copied, 1)
                if has(s, 2):
                    act.wait_ge(nmax_turned, s - 1)
                    nc.scalar.activation(nmax_p[:, :], ps_max[:, P:P + PAIR], ACT.Copy).then_inc(nmax_copied, 1)
                    act.wait_ge(nmax_copied, s - 1)
                    for t in range(PAIR):
                        ins = nc.scalar.activation(ex[:, t, :], kept[:, t * ROWS:(t + 1) * ROWS], ACT.Exp,
                                                   bias=nmax_p[:, t:t + 1])
                    ins.then_inc(exp_done, 1)
                if has(s, 1):
                    sum_products(s - 1, k - 1, 1, "v", 0, VPROD)
                if has(s, 0):
                    act.wait_ge(sum_done, s + 1)
                    if has(s, 1):
                        act.wait_ge(mean_done, s)
                    nc.scalar.activation(sums[:, :], ps_sum[:, 0:2 * D], ACT.Copy, scale=rcnt_rows[:, bass.ds(s, 1)]
                                         ).then_inc(sum_copied, 1)
                if has(s, 1):
                    sum_products(s - 1, k - 1, 0, "g", 0, GCHUNKS[0][1])
                    sum_products(s - 1, k - 1, 0, "g", GCHUNKS[0][1], GPROD)
                if has(s, 0):
                    act.wait_ge(mean_done, s + 1)
                    nc.scalar.activation(mean_p[:, :], c_mean, ACT.Copy).then_inc(mean_copied, 1)
                if has(s, 1):
                    sum_products(s - 1, k - 1, 1, "g", 0, GCHUNKS[0][1])
                if has(s, 0):
                    act.wait_ge(query_done, s + 1)
                    if has(s, 2):
                        act.wait_ge(dots_done, (s - 1) * PAIR)
                        act.wait_ge(gprod_ready, (s - 1) * PAIR * len(GCHUNKS))
                    nc.scalar.activation(query[:, k % 2, :, :].rearrange("p t d -> p (t d)"), c_query, ACT.Copy
                                         ).then_inc(query_ready, 1)
                if has(s, 1):
                    sum_products(s - 1, k - 1, 1, "g", GCHUNKS[0][1], GPROD)

            act.wait_ge(sp_exp_in, 1)
            nc.scalar.activation(soft[:, 1:2], soft[:, 0:1], ACT.Exp).then_inc(sp_exp, 1)
            act.wait_ge(sp_ln_in, 1)
            nc.scalar.activation(soft[:, 3:4], soft[:, 2:3], ACT.Ln).then_inc(sp_ln, 1)
            act.wait_ge(rcnt_spread, 1)
            nc.scalar.activation(rcnt_rows[:, :], ps_fin[:, 0:NPAIR], ACT.Copy).then_inc(rcnt_rows_ready, 1)
            act.wait_ge(rcnt_rows_ready, 1)
            act.wait_ge(gate_in, 1)
            nc.scalar.activation(st[:, 12:14, :], st[:, 10:12, :], ACT.Exp).then_inc(gate_exp, 1)
            step(0, 0)
            act.wait_ge(alpha_ready, 1)
            act.wait_ge(ld_age_p, 16)
            nc.scalar.activation(decay[:, :], age_p[:, :], ACT.Exp, scale=soft[:, 5:6]).then_inc(decay_exp, 1)
            steps(act, step, NPAIR + 2, first=1)

        @block.vector
        def _(dve):
            made = [0]

            def link(ins):
                made[0] += 1
                ins.then_inc(dve_setup, 1)
                dve.wait_ge(dve_setup, made[0])

            V = nc.vector
            CNT, LOW, FIRST, DEN, RDEN, SPOP, SAGE, T0, T1, Z, ZNEG, ZABS, EZNEG, EZABS, GATE, GDIV = (
                st[:, n, :] for n in range(16))

            def setup_early():
                dve.wait_ge(ld_mask_p, 16)
                V.tensor_copy(mask_f[:, :, :], mask_p[:, :, :]).then_inc(mask_ready, 1)
                dve.wait_ge(ld_mask_s, 16)
                link(V.tensor_reduce(rcnt[:, :], mask_s[:, :, :], AX.X, ALU.add))
                link(V.tensor_scalar(rcnt[:, :], rcnt[:, :], 1e-6, None, ALU.add))
                V.reciprocal(rcnt[:, :], rcnt[:, :]).then_inc(rcnt_ready, 1)
                dve.wait_ge(ld_mask_u, 16)
                link(V.tensor_reduce(CNT, mask_u[:, :, :], AX.X, ALU.add))
                link(V.tensor_scalar(CNT, CNT, 1.0, None, ALU.max))
                link(V.tensor_scalar(LOW, CNT, -float(LAST), None, ALU.add))
                link(V.tensor_scalar(FIRST, LOW, 0.0, None, ALU.max))
                dve.wait_ge(pool_setup, POOL_CONSTANTS)
                V.tensor_tensor(first_row[:, :], FIRST, user0[:, :], ALU.add).then_inc(rows_ready, 1)
                dve.wait_ge(wqk_done, 1)
                V.tensor_scalar(wqk[:, :], ps_fin[:, 0:D], SCALE, None, ALU.mult).then_inc(wqk_ready, 1)
                V.tensor_copy(wv_t[:, :], ps_fin[:, 128:256]).then_inc(wqk_ready, 1)

            def setup_decay():
                dve.wait_ge(ld_small, 80)
                V.scalar_tensor_tensor(out=soft[:, 0:1], in0=da[:, :], scalar=-1.0, in1=da[:, :],
                                       op0=ALU.mult, op1=ALU.min).then_inc(sp_exp_in, 1)
                dve.wait_ge(sp_exp, 1)
                V.tensor_scalar(soft[:, 2:3], soft[:, 1:2], 1.0, None, ALU.add).then_inc(sp_ln_in, 1)
                dve.wait_ge(sp_ln, 1)
                link(V.scalar_tensor_tensor(out=soft[:, 4:5], in0=da[:, :], scalar=0.0, in1=soft[:, 3:4],
                                            op0=ALU.max, op1=ALU.add))
                V.tensor_scalar(soft[:, 5:6], soft[:, 4:5], 1e-6, -1.0, ALU.add, ALU.mult).then_inc(alpha_ready, 1)

            def setup_masked_decay():
                dve.wait_ge(mask_ready, 1)
                mp = mask_f[:, :, :].rearrange("p g r -> p (g r)")
                link(V.tensor_scalar(hide[:, :], mp, -1.0, BIG, ALU.add, ALU.mult))
                dve.wait_ge(decay_exp, 1)
                link(V.scalar_tensor_tensor(out=decay[:, :], in0=decay[:, :], scalar=1e-12, in1=mp,
                                            op0=ALU.add, op1=ALU.mult))

            def setup_gate():
                link(V.tensor_scalar(DEN, CNT, float(LAST), None, ALU.min))
                link(V.reciprocal(RDEN, DEN))
                dve.wait_ge(ld_users, 32)
                for q in range(NGROUP):
                    link(V.tensor_scalar(last[:, 0, :], pos[:, :], LOW[:, q:q + 1], None, ALU.is_ge))
                    link(V.scalar_tensor_tensor(out=last[:, 1, :], in0=pos[:, :], scalar=CNT[:, q:q + 1],
                                                in1=last[:, 0, :], op0=ALU.is_lt, op1=ALU.mult))
                    for src, total in ((pop_u, SPOP), (age_u, SAGE)):
                        link(V.scalar_tensor_tensor(out=junk_u[:, :], in0=src[:, q, :], scalar=1.0, in1=last[:, 1, :],
                                                    op0=ALU.mult, op1=ALU.mult, accum_out=total[:, q:q + 1]))
                link(V.tensor_scalar(T0, SPOP, gw[:, 0:1], None, ALU.mult))
                link(V.scalar_tensor_tensor(out=T1, in0=SAGE, scalar=gw[:, 1:2], in1=T0, op0=ALU.mult, op1=ALU.add))
                link(V.tensor_tensor(T0, T1, RDEN, ALU.mult))
                link(V.tensor_scalar(Z, T0, gb[:, 0:1], None, ALU.add))
                link(V.tensor_scalar(ZNEG, Z, 0.0, None, ALU.min))
                V.scalar_tensor_tensor(out=ZABS, in0=Z, scalar=-1.0, in1=Z, op0=ALU.mult, op1=ALU.min
                                       ).then_inc(gate_in, 1)
                dve.wait_ge(gate_exp, 1)
                link(V.tensor_scalar(T0, EZABS, 1.0, None, ALU.add))
                link(V.reciprocal(T1, T0))
                link(V.tensor_tensor(GATE, EZNEG, T1, ALU.mult))
                link(V.tensor_scalar(stay_[:, :], GATE, -1.0, 1.0, ALU.mult, ALU.add))
                link(V.tensor_tensor(GDIV, GATE, RDEN, ALU.mult))
                for i in range(LAST):
                    link(V.scalar_tensor_tensor(out=lw[:, i, :], in0=FIRST, scalar=float(i), in1=CNT,
                                                op0=ALU.add, op1=ALU.is_lt))
                    link(V.tensor_tensor(lw[:, i, :], lw[:, i, :], GDIV, ALU.mult))

            def short_term(g, i):
                w = lw[:, i, bass.ds(g, 1)]
                if i == 0:
                    dve.wait_ge(gathered, g * (16 * LAST) + 16 * LAST)
                    ins = V.tensor_scalar(short[:, :], taken[:, i, :], w, None, ALU.mult)
                else:
                    dve.wait_ge(short_part, g * LAST + i)
                    ins = V.scalar_tensor_tensor(out=short[:, :], in0=taken[:, i, :], scalar=w, in1=short[:, :],
                                                 op0=ALU.mult, op1=ALU.add)
                ins.then_inc(short_part, 1)

            def mask_and_max(s, k):
                dve.wait_ge(vsums_done, s * PAIR + PAIR)
                dve.wait_ge(gsums_done, s * PAIR + PAIR)
                dve.wait_ge(dots_done, s * PAIR + PAIR)
                V.tensor_tensor(kept[:, :], score[:, k % 2, :, :].rearrange("p t r -> p (t r)"),
                                hide[:, bass.ds(s * PROWS, PROWS)], ALU.add).then_inc(kept_ready, 1)
                dve.wait_ge(kept_ready, s + 1)
                V.tensor_reduce(pmax[:, :], kept[:, :].rearrange("p (t r) -> p t r", t=PAIR), AX.X, ALU.max
                                ).then_inc(pmax_ready, 1)

            def user_max(s):
                dve.wait_ge(pmax_turned, s + 1)
                V.tensor_reduce(umax[:, :], ps_max[0:PAIR, 0:P].rearrange("t (u c) -> t u c", c=PU), AX.X, ALU.max
                                ).then_inc(umax_ready, 1)
                dve.wait_ge(umax_ready, s + 1)
                V.tensor_scalar(nmax[:, :].rearrange("t (u c) -> t u c", c=PU),
                                umax[:, :].unsqueeze(2).broadcast_to([PAIR, TU, PU]), -1.0, None, ALU.mult
                                ).then_inc(nmax_ready, 1)

            def weights(s, k):
                dve.wait_ge(exp_done, s + 1)
                if has(s, 1):
                    dve.wait_ge(pblk_ready, s * PAIR)
                for t in range(PAIR):
                    i = (k % GP) * PAIR + t
                    V.scalar_tensor_tensor(out=wts[:, t, :], in0=ex[:, t, :], scalar=1.0,
                                           in1=decay[:, bass.ds(s * PROWS + t * ROWS, ROWS)],
                                           op0=ALU.mult, op1=ALU.mult, accum_out=wsum[:, i:i + 1]).then_inc(wts_ready, 1)

            def products(s, k, t):
                dve.wait_ge(query_ready, s + 1)
                if has(s, 1):
                    dve.wait_ge(vsums_done, (s - 1) * PAIR + t + 1)
                V.tensor_tensor(vprod[:, t, :].rearrange("p (r d) -> p r d", d=D),
                                rows((k % GP) * PAIR + t, DOTS, DOTS + VPROD),
                                query[:, k % 2, t, :].unsqueeze(1).broadcast_to([P, VPROD, D]),
                                ALU.mult).then_inc(vprod_ready, 1)

            def dots(s, k, t, a, b):
                for r in range(a, b):
                    ins = V.scalar_tensor_tensor(out=junk_v[:, t, r, :], in0=x[:, (k % GP) * PAIR + t, r * D:(r + 1) * D],
                                                 scalar=1.0, in1=query[:, k % 2, t, :], op0=ALU.mult, op1=ALU.mult,
                                                 accum_out=score[:, k % 2, t, r:r + 1])
                if a < b == DOTS:
                    ins.then_inc(dots_done, 1)

            def finish_att(g):
                dve.wait_ge(den_done, g)
                V.reciprocal(rden[:, :], ps_fin[:, 0:1]).then_inc(rden_ready, 1)
                dve.wait_ge(rden_ready, g)
                dve.wait_ge(wx_folded, g * GP)
                V.tensor_scalar(att[:, :], ps_group[:, 0:D], rden[:, :], None, ALU.mult).then_inc(att_ready, 1)

            def finish_user(g):
                dve.wait_ge(long_done, g)
                dve.wait_ge(short_part, g * LAST)
                V.scalar_tensor_tensor(out=user[:, :], in0=ps_fin[:, 256:384], scalar=stay_[:, bass.ds(g - 1, 1)],
                                       in1=short[:, :], op0=ALU.mult, op1=ALU.add).then_inc(user_ready, 1)

            def finish_stats(g):
                dve.wait_ge(user_ready, g)
                V.bn_stats(bn[:, :], user[:, :]).then_inc(bn_ready, 1)

            def finish_moments(g):
                dve.wait_ge(bn_ready, g)
                dve.sem_inc(dve_passed, 1)
                V.bn_aggr(mv[:, :], bn[:, :]).then_inc(mv_ready, 1)

            def finish_variance(g):
                dve.wait_ge(mv_ready, g)
                V.tensor_scalar(vare[:, :], mv[:, 1:2], 1e-5, None, ALU.add).then_inc(var_ready, 1)

            def finish_centre(g):
                dve.wait_ge(rstd_ready, g)
                V.tensor_scalar(y0[:, :], user[:, :], mv[:, 0:1], rstd[:, :], ALU.subtract, ALU.mult
                                ).then_inc(norm_ready, 1)

            def finish_scale(g):
                dve.wait_ge(norm_ready, g)
                V.tensor_tensor(y1[:, :], y0[:, :], gam[:, :], ALU.mult).then_inc(scaled_ready, 1)

            def finish_shift(g):
                dve.wait_ge(scaled_ready, g)
                V.tensor_tensor(y[:, bass.ds(g - 1, 1), :].rearrange("p q d -> p (q d)"), y1[:, :], bet[:, :], ALU.add
                                ).then_inc(y_ready, 1)

            def step(g, k):
                s = g * GP + k
                fin = has(g, 1, NGROUP)
                if has(s, 1):
                    products(s - 1, k - 1, 0)
                    products(s - 1, k - 1, 1)
                if has(s, 2):
                    mask_and_max(s - 2, k)
                if k == 3 and fin:
                    dve.wait_ge(att_turned, g)
                    V.tensor_copy(att_t[:, :], ps_fin[:, 128:256]).then_inc(att_t_ready, 1)
                if has(s, 1):
                    dots(s - 1, k - 1, 0, 0, 3)
                if has(s, 2):
                    user_max(s - 2)
                if has(s, 1):
                    dots(s - 1, k - 1, 0, 3, 10)
                if has(s, 2):
                    weights(s - 2, k - 2)
                if k == 1 and fin:
                    dve.wait_ge(wts_ready, (s - 1) * PAIR)
                    V.tensor_tensor(wsum_blk[:, :, :], own[:, :].unsqueeze(1).broadcast_to([P, GP * PAIR, TU]),
                                    wsum[:, :].unsqueeze(2).broadcast_to([P, GP * PAIR, TU]), ALU.mult
                                    ).then_inc(wsum_ready, 1)
                if k == 0 and fin:
                    for i in range(LAST):
                        short_term(g - 1, i)
                        if has(s, 1):
                            dots(s - 1, k - 1, 0, 10 + i, min(11 + i, DOTS))
                elif k == 2 and fin:
                    finish_att(g)
                    dots(s - 1, k - 1, 0, 10, DOTS) if has(s, 1) else None
                elif k == 3 and fin:
                    for i, part in enumerate((finish_user, finish_stats, finish_moments, finish_variance)):
                        part(g)
                        if has(s, 1):
                            dots(s - 1, k - 1, 0, 10 + i, min(11 + i, DOTS))
                elif has(s, 1):
                    dots(s - 1, k - 1, 0, 10, DOTS)
                if k == 3 and fin:
                    if has(s, 1):
                        dots(s - 1, k - 1, 1, 0, DOTS - 6)
                    for i, part in enumerate((finish_centre, finish_scale, finish_shift)):
                        part(g)
                        if has(s, 1):
                            dots(s - 1, k - 1, 1, DOTS - 6 + 2 * i, DOTS - 4 + 2 * i)
                elif has(s, 1):
                    dots(s - 1, k - 1, 1, 0, DOTS)

            setup_early()
            setup_decay()
            setup_gate()
            step(0, 0)
            setup_masked_decay()
            steps(dve, step, NPAIR + 3, first=1)

    return nc


def kernel(**inputs):
    import numpy as _np
    import concourse.bacc as _bacc
    from concourse.bass_utils import run_bass_kernel_spmd as _run

    names = ["r_hist_items", "r_hist_mask", "r_hist_age_hours", "r_hist_popularity", "L0_rec_Wq", "L0_rec_Wk",
             "L0_rec_Wv", "L0_rec_gate_w", "L0_rec_gate_b", "L0_rec_ln_gamma", "L0_rec_ln_beta", "L0_rec_decay_alpha"]
    nc = _bacc.Bacc("TRN2", target_bir_lowering=False, num_devices=1)
    arrays, args = {}, []
    for name in names:
        a = _np.ascontiguousarray(inputs[name])
        arrays[f"in_{name}_dram"] = a
        args.append(nc.dram_tensor(f"in_{name}_dram", a.shape, mybir.dt.from_np(a.dtype), kind="ExternalInput").ap())
    out = nc.dram_tensor("out_dram", (NUSER, D), F32, kind="ExternalOutput").ap()
    build(nc, *args, out)
    r = _run(nc, [arrays], core_ids=[0])
    return r.results[0]["out_dram"]
```

```python
import concourse.bass as bass
from concourse import mybir
from concourse.alu_op_type import AluOpType as ALU
from contextlib import ExitStack

F32 = mybir.dt.float32
U8 = mybir.dt.uint8
I32 = mybir.dt.int32
U32 = mybir.dt.uint32
ACT = mybir.ActivationFunctionType
AX = mybir.AxisListType

NUSER, NITEM, D = 512, 200, 128
P = 128
LAST = 5
PU = 8
ROWS = NITEM // PU
TU = P // PU
NTILE = NUSER // TU
PAIR = 2
NPAIR = NTILE // PAIR
GP = 4
NGROUP = NPAIR // GP
SLOTS = GP * PAIR
PROWS = PAIR * ROWS
CG = 4
PUSERS = PAIR * TU
NPROD = (ROWS + 1) // 2
CUT_SUMS, CUT_MEAN = 5, 10
KEPT_AT, USER_MAX_AT, WEIGHTS_AT = 8, 13, 12
BIG = 3.0e38
SCALE = float(D) ** -0.5

DOTS = 15
VPROD = 4
GPROD = ROWS - DOTS - VPROD
GCHUNKS = ((0, GPROD // 2), (GPROD // 2, GPROD))
POOL_IDENT = 5
POOL_CONSTANTS = 15


def build(nc, items, mask, age, pop, Wq, Wk, Wv, gate_w, gate_b, gamma, beta, decay_alpha, out):
    items_t = items.rearrange("u t d -> (u t d)").rearrange("(g p n) -> g p n", p=P, n=ROWS * D)
    items_rows = items.rearrange("u t d -> (u t) d")
    mask_t = mask.rearrange("u t -> (u t)").rearrange("(g p r) -> p g r", p=P, r=ROWS)
    age_t = age.rearrange("u t -> (u t)").rearrange("(g p r) -> p g r", p=P, r=ROWS)
    mask_n, age_n, pop_n = (a.rearrange("(q u) t -> u q t", u=P) for a in (mask, age, pop))

    ctx = ExitStack()
    with ctx:
        def sb(name, shape, dt=F32):
            return ctx.enter_context(nc.sbuf_tensor(name, shape, dt))

        def bank(name):
            return ctx.enter_context(nc.psum_tensor(name, [P, 512], F32))

        def sem(name):
            return ctx.enter_context(nc.semaphore(name))

        x = sb("x", [P, SLOTS, ROWS * D])
        wq, wk, wv = sb("wq", [P, D]), sb("wk", [P, D]), sb("wv", [P, D])
        wqk, wv_t = sb("wqk", [P, D]), sb("wv_t", [P, D])
        ident = sb("ident", [P, P])
        ones = sb("ones", [P, 1])
        own = sb("own", [P, TU])
        fold = sb("fold", [P, 2, TU])
        own_rows = sb("own_rows", [P, CG * 2, TU])
        gam, bet = sb("gam", [P, D]), sb("bet", [P, D])
        gw, gb, da = sb("gw", [P, 2]), sb("gb", [P, 1]), sb("da", [P, 1])
        mask_p = sb("mask_p", [P, NTILE, ROWS], U8)
        mask_f = sb("mask_f", [P, NTILE, ROWS])
        mask_u = sb("mask_u", [P, NGROUP, NITEM], U8)
        age_p = sb("age_p", [P, NTILE * ROWS])
        decay = sb("decay", [P, NTILE * ROWS])
        hide = sb("hide", [P, NTILE * ROWS])
        age_u, pop_u = sb("age_u", [P, NGROUP, NITEM]), sb("pop_u", [P, NGROUP, NITEM])
        pos = sb("pos", [P, NITEM])
        cnt_p = sb("cnt_p", [P, NTILE])
        st = sb("st", [P, 16, NGROUP])
        soft = sb("soft", [P, 8])
        stay_ = sb("stay", [P, NGROUP])
        last = sb("last", [P, 2, NITEM])
        junk_u = sb("junk_u", [P, NITEM])
        junk_v = sb("junk_v", [P, PAIR, DOTS, D])
        first_row = sb("first_row", [P, NGROUP], U32)
        user0 = sb("user0", [P, NGROUP])
        group_row = sb("group_row", [P, 1], U32)
        taken = sb("taken", [P, LAST, D])
        lw = sb("lw", [P, LAST, NGROUP])
        short = sb("short", [P, D])
        mblk = sb("mblk", [P, 2, PAIR, ROWS, TU])
        pblk = sb("pblk", [P, 2, PAIR, ROWS, TU])
        sums = sb("sums", [P, PAIR, 2 * D])
        cnt_rows = sb("cnt_rows", [P, NTILE])
        rcnt_rows = sb("rcnt_rows", [P, NTILE])
        mean_p = sb("mean_p", [P, PAIR, TU, PU])
        query = sb("query", [P, 2, PAIR, D])
        vprod = sb("vprod", [P, PAIR, VPROD * D])
        gprod = sb("gprod", [P, PAIR, GPROD * D])
        score = sb("score", [P, 2, PAIR, ROWS])
        kept = sb("kept", [P, PROWS])
        pmax = sb("pmax", [P, PAIR])
        umax = sb("umax", [PAIR, TU])
        nmax = sb("nmax", [PAIR, P])
        nmax_p = sb("nmax_p", [P, PAIR])
        ex = sb("ex", [P, PAIR, ROWS])
        wts = sb("wts", [P, PAIR, ROWS])
        wsum = sb("wsum", [P, GP * PAIR])
        wsum_blk = sb("wsum_blk", [P, GP * PAIR, TU])
        wx = sb("wx", [P, PAIR, 2 * D])
        rden, long_scale = sb("rden", [P, 1]), sb("long_scale", [P, 1])
        att_t = sb("att_t", [P, P])
        user = sb("user", [P, D])
        bn = sb("bn", [P, 6])
        mv = sb("mv", [P, 2])
        vare, half, rstd = sb("vare", [P, 1]), sb("half", [P, 1]), sb("rstd", [P, 1])
        centred = sb("centred", [P, D])
        y = sb("y", [P, NGROUP, D])

        ps_sum = bank("ps_sum0"), bank("ps_sum1")
        ps_chain = bank("ps_chain")
        ps_max = bank("ps_max")
        ps_wx = bank("ps_wx0"), bank("ps_wx1")
        ps_group = bank("ps_group")
        ps_fin = bank("ps_fin")
        c_mean = ps_chain[:, 256:256 + TU]
        c_query = ps_chain[:, 0:D]

        x_loaded = [sem(f"x_loaded{i}") for i in range(SLOTS)]
        ld_weights, ld_mask_p = sem("ld_weights"), sem("ld_mask_p")
        ld_mask_u, ld_age_p, ld_users, ld_small = sem("ld_mask_u"), sem("ld_age_p"), sem("ld_users"), sem("ld_small")
        pool_setup, dve_setup, act_setup = sem("pool_setup"), sem("dve_setup"), sem("act_setup")
        wqk_done, wqk_ready = sem("wqk_done"), sem("wqk_ready")
        sp_exp_in, sp_exp, sp_ln_in, sp_ln, alpha_ready, decay_exp = (
            sem("sp_exp_in"), sem("sp_exp"), sem("sp_ln_in"), sem("sp_ln"), sem("alpha_ready"), sem("decay_exp"))
        gate_in, gate_exp, rows_ready = sem("gate_in"), sem("gate_exp"), sem("rows_ready")
        short_part = sem("short_part")
        row_copied, gathered = sem("row_copied"), sem("gathered")
        mask_ready = sem("mask_ready")
        mblk_ready = sem("mblk_ready")
        sum_done, sum_copied = sem("sum_done"), sem("sum_copied")
        cnt_ready, cnt_spread, rcnt_rows_ready = sem("cnt_ready"), sem("cnt_spread"), sem("rcnt_rows_ready")
        mean_done, mean_copied = sem("mean_done"), sem("mean_copied")
        query_done, query_ready = sem("query_done"), sem("query_ready")
        vprod_ready, gprod_ready = sem("vprod_ready"), sem("gprod_ready")
        dots_done, vsums_done, gsums_done = sem("dots_done"), sem("vsums_done"), sem("gsums_done")
        kept_ready, pmax_ready, pmax_turned = sem("kept_ready"), sem("pmax_ready"), sem("pmax_turned")
        umax_ready, nmax_ready, nmax_turned = sem("umax_ready"), sem("nmax_ready"), sem("nmax_turned")
        nmax_copied = sem("nmax_copied")
        exp_done, wts_ready, pblk_ready = sem("exp_done"), sem("wts_ready"), sem("pblk_ready")
        wx_done, wx_copied, wx_folded = sem("wx_done"), sem("wx_copied"), sem("wx_folded")
        wsum_ready, den_done, rden_ready, scale_ready = (
            sem("wsum_ready"), sem("den_done"), sem("rden_ready"), sem("scale_ready"))
        att_t_ready, long_done = sem("att_t_ready"), sem("long_done")
        user_ready, bn_ready, mv_ready, var_ready = sem("user_ready"), sem("bn_ready"), sem("mv_ready"), sem("var_ready")
        rstd_ready, centred_ready, y_ready = sem("rstd_ready"), sem("centred_ready"), sem("y_ready")
        pe_passed, pool_passed, dve_passed = sem("pe_passed"), sem("pool_passed"), sem("dve_passed")
        y_stored = sem("y_stored")

        block = ctx.enter_context(nc.Block())

        def steps(eng, step, last_step, first=0, groups=NGROUP):
            for k in range(first, GP):
                step(0, k)
            with eng.Fori(1, groups) as g:
                for k in range(GP):
                    step(g, k)
            for s in range(groups * GP, last_step + 1):
                step(s // GP, s % GP)

        def has(s, back, n=NPAIR):
            return not isinstance(s, int) or 0 <= s - back < n

        def rows(i, a, b):
            return x[:, i, a * D:b * D].rearrange("p (r d) -> p r d", d=D)

        @block.sync
        def _(sp):
            def store(q):
                sp.wait_ge(y_ready, q + 1)
                sp.dma_start(out[bass.ds(q * P, P), :], y[:, bass.ds(q, 1), :].rearrange("p q d -> p (q d)")
                             ).then_inc(y_stored, 16)

            def load(s, k, t):
                i = k * PAIR + t
                sp.dma_start(x[:, i, :], items_t[bass.ds(s * PAIR + t, 1), :, :].rearrange("g p n -> (g p) n")
                             ).then_inc(x_loaded[i], 16)

            def step(g, k):
                s = g * GP + k
                for t in range(PAIR):
                    if has(s, GP):
                        sp.wait_ge(wx_done, (s - GP) * PAIR + t + 1)
                    load(s, k, t)

            sp.dma_start(mask_p[:, :, :], mask_t).then_inc(ld_mask_p, 16)
            for dst, src in ((wq, Wq), (wk, Wk), (wv, Wv)):
                sp.dma_start(dst[:, :], src).then_inc(ld_weights, 16)
            sp.dma_start(mask_u[:, :, :], mask_n).then_inc(ld_mask_u, 16)
            load(0, 0, 0)
            sp.dma_start(gw[:, :], gate_w.broadcast_to([P, 2])).then_inc(ld_small, 16)
            for dst, src in ((da, decay_alpha), (gb, gate_b), (gam, gamma), (bet, beta)):
                sp.dma_start(dst[:, :], src.unsqueeze(0).broadcast_to([P, src.shape[0]])).then_inc(ld_small, 16)
            sp.dma_start(pop_u[:, :, :], pop_n).then_inc(ld_users, 16)
            sp.dma_start(age_u[:, :, :], age_n).then_inc(ld_users, 16)
            load(0, 0, 1)
            sp.dma_start(age_p[:, :].rearrange("p (g r) -> p g r", r=ROWS), age_t).then_inc(ld_age_p, 16)
            steps(sp, step, NPAIR - 1, first=1)
            for q in range(NGROUP):
                store(q)
            sp.wait_ge(y_stored, 16 * NGROUP)

        @block.gpsimd
        def _(pool):
            made = [0]

            def link(ins):
                made[0] += 1
                ins.then_inc(pool_setup, 1)
                pool.wait_ge(pool_setup, made[0])

            def select(ap, op, pattern, base, mult, fill):
                link(nc.gpsimd.affine_select(out=ap, in_=ap, compare_op=op, fill=fill, base=base,
                                             pattern=pattern, channel_multiplier=mult))

            def build_mblk(s, k):
                for t in range(PAIR):
                    if has(s, 2):
                        pool.wait_ge(sum_done, (s - 2) * PAIR + t + 1)
                    m = mask_f[:, bass.ds(s * PAIR + t, 1), :].rearrange("p g r -> p (g r)")
                    nc.gpsimd.tensor_tensor(mblk[:, k % 2, t, :, :], own[:, :].unsqueeze(1).broadcast_to([P, ROWS, TU]),
                                            m.unsqueeze(2).broadcast_to([P, ROWS, TU]), ALU.mult).then_inc(mblk_ready, 1)

            def build_pblk(s, k):
                for t in range(PAIR):
                    pool.wait_ge(wts_ready, s * PAIR + t + 1)
                    if has(s, 2):
                        pool.wait_ge(wx_done, (s - 2) * PAIR + t + 1)
                    nc.gpsimd.tensor_tensor(pblk[:, k % 2, t, :, :], own[:, :].unsqueeze(1).broadcast_to([P, ROWS, TU]),
                                            wts[:, t, :].unsqueeze(2).broadcast_to([P, ROWS, TU]), ALU.mult
                                            ).then_inc(pblk_ready, 1)

            def products(s, k, t):
                pool.wait_ge(query_ready, s * PAIR + t + 1)
                if has(s, 1):
                    pool.wait_ge(gsums_done, (s - 1) * PAIR + t + 1)
                r0 = DOTS + VPROD
                for a, b in GCHUNKS:
                    nc.gpsimd.tensor_tensor(gprod[:, t, a * D:b * D].rearrange("p (r d) -> p r d", d=D),
                                            rows((k % GP) * PAIR + t, r0 + a, r0 + b),
                                            query[:, k % 2, t, :].unsqueeze(1).broadcast_to([P, b - a, D]),
                                            ALU.mult).then_inc(gprod_ready, 1)

            def inverse_deviation(q):
                pool.wait_ge(var_ready, q + 1)
                nc.gpsimd.tensor_tensor(rstd[:, :], vare[:, :], half[:, :], ALU.pow).then_inc(rstd_ready, 1)

            link(nc.gpsimd.memset(own[:, :], 1.0))
            select(own[:, :], ALU.is_ge, [[-PU, TU]], 0, 1, 0.0)
            select(own[:, :], ALU.is_ge, [[PU, TU]], PU - 1, -1, 0.0)
            link(nc.gpsimd.memset(ident[:, :], 0.0))
            select(ident[:, :], ALU.not_equal, [[-1, P]], 0, 1, 1.0)
            link(nc.gpsimd.tensor_copy(own_rows[:, :, :], own[:, :].unsqueeze(1).broadcast_to([P, CG * 2, TU])))
            pool.wait_ge(mask_ready, 1)
            build_mblk(0, 0)
            link(nc.gpsimd.memset(fold[:, :, :].rearrange("p a u -> p (a u)"), 0.0))
            for c in range(CG):
                select(fold[:, :, :], ALU.not_equal, [[-TU, 2], [-1, TU]], -32 * c, 1, 1.0)
            link(nc.gpsimd.iota(pos[:, :], [[1, NITEM]], base=0, channel_multiplier=0,
                                allow_small_or_imprecise_dtypes=True))
            link(nc.gpsimd.iota(user0[:, :], [[NITEM * P, NGROUP]], base=0, channel_multiplier=NITEM,
                                allow_small_or_imprecise_dtypes=True))
            link(nc.gpsimd.memset(ones[:, :], 1.0))
            link(nc.gpsimd.memset(half[:, :], -0.5))
            def gather(g):
                if has(g, 1):
                    pool.wait_ge(short_part, g * LAST)
                nc.gpsimd.tensor_copy(group_row[:, :], first_row[:, bass.ds(g, 1)]).then_inc(row_copied, 1)
                pool.wait_ge(row_copied, g + 1)
                pool.sem_inc(pool_passed, 1)
                nc.gpsimd.indirect_dma_start(
                    out=taken[:, :, :].rearrange("p i d -> p (i d)"), out_offset=None, in_=items_rows,
                    in_offset=bass.IndirectOffsetOnAxis(ap=group_row[:, :], axis=0)).then_inc(gathered, 16)

            def step(g, k):
                s = g * GP + k
                if has(s, 1):
                    products(s - 1, k - 1, 1)
                if has(s, -1):
                    build_mblk(s + 1, k + 1)
                if has(s, 2):
                    build_pblk(s - 2, k - 2)
                if has(s, 0):
                    products(s, k, 0)
                if k == 0 and has(s, 0):
                    gather(g)
                if k == 3 and has(g, 1, NGROUP):
                    inverse_deviation(g - 1)

            pool.wait_ge(rows_ready, 1)
            steps(pool, step, NPAIR + 3, groups=NGROUP - 1)
            assert made[0] == POOL_CONSTANTS

        @block.tensor
        def _(pe):
            def sum_rows(dst, blk, i, k, t, ms=range(NPROD)):
                for m in ms:
                    n = min(2, ROWS - 2 * m)
                    c = 32 * (m % CG)
                    ins = nc.tensor.matmul(dst[c:c + n * TU, 0:n * D],
                                           blk[:, k % 2, t, 2 * m:2 * m + n, :].rearrange("p r u -> p (r u)"),
                                           x[:, i + t, 2 * m * D:(2 * m + n) * D],
                                           start=(m < CG), stop=(m >= NPROD - CG))
                return ins

            def make_mean(s, t):
                pe.wait_ge(sum_copied, s * PAIR + t + 1)
                if t > 0 or has(s, 1):
                    pe.wait_ge(query_ready, s * PAIR + t)
                for rr in range(2):
                    ins = nc.tensor.matmul(c_mean, sums[:, t, rr * D:(rr + 1) * D], fold[:, rr, :],
                                           start=(rr == 0), stop=(rr == 1))
                ins.then_inc(mean_done, 1)

            def make_query(s, t):
                pe.wait_ge(mean_copied, s * PAIR + t + 1)
                nc.tensor.matmul(c_query, mean_p[:, t, :, :].rearrange("p u c -> p (u c)"), wqk[:, :],
                                 start=True, stop=True).then_inc(query_done, 1)

            def fold_rows(s, c, src):
                for t in range(PAIR):
                    pe.wait_ge(wx_copied, s * PAIR + t + 1)
                    for rr in range(2):
                        ins = nc.tensor.matmul(ps_group[:, c + t * TU:c + (t + 1) * TU], src[:, t, rr * D:(rr + 1) * D],
                                               fold[:, rr, :], start=(rr == 0), stop=(rr == 1))
                return ins

            def masked_sums(s, g, k, t):
                pe.wait_ge(x_loaded[k * PAIR + t], g * 16 + 16)
                pe.wait_ge(mblk_ready, s * PAIR + t + 1)
                if has(s, 1):
                    pe.wait_ge(sum_copied, (s - 1) * PAIR + t + 1)
                sum_rows(ps_sum[t], mblk, k * PAIR, k, t).then_inc(sum_done, 1)

            def weighted_sums(s, k, t, ms=range(NPROD)):
                if ms[0] == 0:
                    pe.wait_ge(pblk_ready, s * PAIR + t + 1)
                    if has(s, 1):
                        pe.wait_ge(wx_copied, (s - 1) * PAIR + t + 1)
                ins = sum_rows(ps_wx[t], pblk, (k % GP) * PAIR, k, t, ms)
                if ms[-1] == NPROD - 1:
                    ins.then_inc(wx_done, 1)

            def turn_max(s):
                pe.wait_ge(pmax_ready, s + 1)
                if has(s, 1):
                    pe.wait_ge(exp_done, s)
                nc.tensor.transpose(ps_max[0:PAIR, 0:P], pmax[:, :], ident[:, :]).then_inc(pmax_turned, 1)

            def turn_user_max(s):
                pe.wait_ge(nmax_ready, s + 1)
                pe.sem_inc(pe_passed, 1)
                nc.tensor.transpose(ps_max[:, P:P + PAIR], nmax[:, :], ident[0:PAIR, 0:PAIR]).then_inc(nmax_turned, 1)

            def step(g, k):
                s = g * GP + k
                for t in range(PAIR):
                    back, u = (3, 1) if t == 0 else (2, 0)
                    if has(s, 0):
                        masked_sums(s, g, k, t)
                    if t == 0 and has(s, 2):
                        turn_user_max(s - 2)
                    if t == 1 and has(s, 3):
                        if k == 3 and has(g, 1):
                            pe.wait_ge(att_t_ready, g)
                        fold_rows(s - 3, PUSERS * ((k - 3) % GP), wx).then_inc(wx_folded, 1)
                    if has(s, back):
                        weighted_sums(s - back, k - back, u, range(CUT_SUMS))
                    if has(s, 0):
                        make_mean(s, t)
                    if has(s, back):
                        weighted_sums(s - back, k - back, u, range(CUT_SUMS, CUT_MEAN))
                    if t == 1 and has(s, 1):
                        turn_max(s - 1)
                    if has(s, 0):
                        make_query(s, t)
                    if has(s, back):
                        weighted_sums(s - back, k - back, u, range(CUT_MEAN, NPROD))
                    if t == 0 and k == 2 and has(g, 1, NGROUP):
                        pe.wait_ge(wsum_ready, g)
                        nc.tensor.matmul(ps_fin[:, 0:1], wsum_blk[:, :, :].rearrange("p t u -> p (t u)"), ones[:, :],
                                         start=True, stop=True).then_inc(den_done, 1)
                    if t == 0 and k == 3 and has(g, 1, NGROUP):
                        pe.wait_ge(att_t_ready, g)
                        nc.tensor.matmul(ps_fin[:, 256:384], att_t[:, :], wv_t[:, :], start=True, stop=True
                                         ).then_inc(long_done, 1)

            pe.wait_ge(ld_weights, 48)
            pe.wait_ge(pool_setup, POOL_IDENT)
            nc.tensor.matmul(ps_fin[:, 0:D], wq[:, :], wk[:, :], start=True, stop=True)
            nc.tensor.transpose(ps_fin[:, 128:256], wv[:, :], ident[:, :]).then_inc(wqk_done, 1)
            pe.wait_ge(pool_setup, POOL_CONSTANTS)
            pe.wait_ge(wqk_ready, 2)
            pe.wait_ge(cnt_ready, 1)
            nc.tensor.matmul(ps_fin[:, 0:NTILE], own_rows[:, :, :].rearrange("p c u -> p (c u)"), cnt_p[:, :],
                             start=True, stop=True).then_inc(cnt_spread, 1)
            steps(pe, step, NPAIR + 3)

        @block.scalar
        def _(act):
            def sum_products(s, k, t, which, a, b):
                prod, r0, n = (vprod, DOTS, VPROD) if which == "v" else (gprod, DOTS + VPROD, GPROD)
                if which == "v" and a == 0:
                    act.wait_ge(vprod_ready, s * PAIR + t + 1)
                    if has(s, 2):
                        act.wait_ge(kept_ready, s - 1)
                if which == "g":
                    act.wait_ge(gprod_ready, (s * PAIR + t) * len(GCHUNKS) + (1 if b <= GCHUNKS[0][1] else 2))
                for r in range(a, b):
                    src = prod[:, t, r * D:(r + 1) * D]
                    ins = nc.scalar.activation(src, src, ACT.Copy, accum_out=score[:, k % 2, t, r0 + r:r0 + r + 1])
                if b == n:
                    ins.then_inc(vsums_done if which == "v" else gsums_done, 1)

            def copy_sums(s, t):
                act.wait_ge(sum_done, s * PAIR + t + 1)
                if has(s, 1):
                    act.wait_ge(mean_done, (s - 1) * PAIR + t + 1)
                nc.scalar.activation(sums[:, t, :], ps_sum[t][:, 0:2 * D], ACT.Copy,
                                     scale=rcnt_rows[:, bass.ds(s * PAIR + t, 1)]).then_inc(sum_copied, 1)

            def copy_weighted(s, t):
                if t == 0 and has(s, 1):
                    act.wait_ge(wx_folded, s)
                act.wait_ge(wx_done, s * PAIR + t + 1)
                nc.scalar.activation(wx[:, t, :], ps_wx[t][:, 0:2 * D], ACT.Copy).then_inc(wx_copied, 1)

            def copy_mean(s, t):
                act.wait_ge(mean_done, s * PAIR + t + 1)
                nc.scalar.activation(mean_p[:, t, :, :], c_mean.unsqueeze(2).broadcast_to([P, TU, PU]), ACT.Copy
                                     ).then_inc(mean_copied, 1)

            def copy_query(s, k, t):
                act.wait_ge(query_done, s * PAIR + t + 1)
                if has(s, 2):
                    act.wait_ge(dots_done, (s - 2) * PAIR + t + 1)
                    act.wait_ge(gprod_ready, ((s - 2) * PAIR + t + 1) * len(GCHUNKS))
                nc.scalar.activation(query[:, k % 2, t, :], c_query, ACT.Copy).then_inc(query_ready, 1)

            def exponentials(s):
                act.wait_ge(nmax_turned, s + 1)
                nc.scalar.activation(nmax_p[:, :], ps_max[:, P:P + PAIR], ACT.Copy).then_inc(nmax_copied, 1)
                act.wait_ge(nmax_copied, s + 1)
                for t in range(PAIR):
                    ins = nc.scalar.activation(ex[:, t, :], kept[:, t * ROWS:(t + 1) * ROWS], ACT.Exp,
                                               bias=nmax_p[:, t:t + 1])
                ins.then_inc(exp_done, 1)

            def step(g, k):
                s = g * GP + k
                if has(s, 0):
                    copy_sums(s, 0)
                if has(s, 2) and not has(s, 0):
                    exponentials(s - 2)
                if has(s, 1):
                    sum_products(s - 1, k - 1, 1, "v", 0, 2)
                if has(s, 0):
                    copy_mean(s, 0)
                if has(s, 2) and has(s, 0):
                    exponentials(s - 2)
                if has(s, 1):
                    sum_products(s - 1, k - 1, 1, "v", 2, VPROD)
                if has(s, 0):
                    copy_query(s, k, 0)
                if has(s, 3) and not has(s, 0):
                    copy_weighted(s - 3, 1)
                if has(s, 1):
                    sum_products(s - 1, k - 1, 1, "g", 0, GCHUNKS[0][1])
                if has(s, 3) and has(s, 0):
                    copy_weighted(s - 3, 1)
                if has(s, 1):
                    sum_products(s - 1, k - 1, 1, "g", GCHUNKS[0][1], GPROD)
                if has(s, 0):
                    copy_sums(s, 1)
                    sum_products(s, k, 0, "v", 0, 2)
                    copy_mean(s, 1)
                    sum_products(s, k, 0, "v", 2, VPROD)
                    copy_query(s, k, 1)
                    sum_products(s, k, 0, "g", 0, GCHUNKS[0][1])
                if has(s, 2):
                    copy_weighted(s - 2, 0)
                if has(s, 0):
                    sum_products(s, k, 0, "g", GCHUNKS[0][1], GPROD)

            act.wait_ge(sp_exp_in, 1)
            nc.scalar.activation(soft[:, 1:2], soft[:, 0:1], ACT.Exp).then_inc(sp_exp, 1)
            act.wait_ge(sp_ln_in, 1)
            nc.scalar.activation(soft[:, 3:4], soft[:, 2:3], ACT.Ln).then_inc(sp_ln, 1)
            act.wait_ge(rcnt_rows_ready, 1)
            step(0, 0)
            act.wait_ge(gate_in, 1)
            nc.scalar.activation(st[:, 12:14, :], st[:, 10:12, :], ACT.Exp).then_inc(gate_exp, 1)
            act.wait_ge(alpha_ready, 1)
            act.wait_ge(ld_age_p, 16)
            nc.scalar.activation(decay[:, :], age_p[:, :], ACT.Exp, scale=soft[:, 5:6]).then_inc(decay_exp, 1)
            steps(act, step, NPAIR + 2, first=1)

        @block.vector
        def _(dve):
            made = [0]

            def link(ins):
                made[0] += 1
                ins.then_inc(dve_setup, 1)
                dve.wait_ge(dve_setup, made[0])

            V = nc.vector
            CNT, LOW, FIRST, DEN, RDEN, SPOP, SAGE, T0, T1, Z, ZNEG, ZABS, EZNEG, EZABS, GATE, GDIV = (
                st[:, n, :] for n in range(16))

            def setup_early():
                dve.wait_ge(ld_mask_p, 16)
                V.tensor_copy(mask_f[:, :, :], mask_p[:, :, :]).then_inc(mask_ready, 1)
                V.tensor_reduce(cnt_p[:, :], mask_p[:, :, :], AX.X, ALU.add).then_inc(cnt_ready, 1)
                dve.wait_ge(ld_mask_u, 16)
                link(V.tensor_reduce(CNT, mask_u[:, :, :], AX.X, ALU.add))
                link(V.tensor_scalar(CNT, CNT, 1.0, None, ALU.max))
                link(V.tensor_scalar(LOW, CNT, -float(LAST), None, ALU.add))
                link(V.tensor_scalar(FIRST, LOW, 0.0, None, ALU.max))
                dve.wait_ge(pool_setup, POOL_CONSTANTS)
                V.tensor_tensor(first_row[:, :], FIRST, user0[:, :], ALU.add).then_inc(rows_ready, 1)
                dve.wait_ge(wqk_done, 1)
                V.tensor_scalar(wqk[:, :], ps_fin[:, 0:D], SCALE, None, ALU.mult).then_inc(wqk_ready, 1)
                V.tensor_copy(wv_t[:, :], ps_fin[:, 128:256]).then_inc(wqk_ready, 1)
                dve.wait_ge(cnt_spread, 1)
                link(V.tensor_scalar(cnt_rows[:, :], ps_fin[:, 0:NTILE], 1e-6, None, ALU.add))
                V.reciprocal(rcnt_rows[:, :], cnt_rows[:, :]).then_inc(rcnt_rows_ready, 1)

            def setup_decay():
                dve.wait_ge(ld_small, 80)
                V.scalar_tensor_tensor(out=soft[:, 0:1], in0=da[:, :], scalar=-1.0, in1=da[:, :],
                                       op0=ALU.mult, op1=ALU.min).then_inc(sp_exp_in, 1)
                dve.wait_ge(sp_exp, 1)
                V.tensor_scalar(soft[:, 2:3], soft[:, 1:2], 1.0, None, ALU.add).then_inc(sp_ln_in, 1)
                dve.wait_ge(sp_ln, 1)
                link(V.scalar_tensor_tensor(out=soft[:, 4:5], in0=da[:, :], scalar=0.0, in1=soft[:, 3:4],
                                            op0=ALU.max, op1=ALU.add))
                V.tensor_scalar(soft[:, 5:6], soft[:, 4:5], 1e-6, -1.0, ALU.add, ALU.mult).then_inc(alpha_ready, 1)

            def setup_hide():
                dve.wait_ge(mask_ready, 1)
                mp = mask_f[:, :, :].rearrange("p g r -> p (g r)")
                link(V.tensor_scalar(hide[:, :], mp, -1.0, BIG, ALU.add, ALU.mult))

            def setup_masked_decay():
                mp = mask_f[:, :, :].rearrange("p g r -> p (g r)")
                dve.wait_ge(decay_exp, 1)
                link(V.scalar_tensor_tensor(out=decay[:, :], in0=decay[:, :], scalar=1e-12, in1=mp,
                                            op0=ALU.add, op1=ALU.mult))

            def setup_gate():
                link(V.tensor_scalar(DEN, CNT, float(LAST), None, ALU.min))
                link(V.reciprocal(RDEN, DEN))
                dve.wait_ge(ld_users, 32)
                for q in range(NGROUP):
                    link(V.tensor_scalar(last[:, 0, :], pos[:, :], LOW[:, q:q + 1], None, ALU.is_ge))
                    link(V.scalar_tensor_tensor(out=last[:, 1, :], in0=pos[:, :], scalar=CNT[:, q:q + 1],
                                                in1=last[:, 0, :], op0=ALU.is_lt, op1=ALU.mult))
                    for src, total in ((pop_u, SPOP), (age_u, SAGE)):
                        link(V.scalar_tensor_tensor(out=junk_u[:, :], in0=src[:, q, :], scalar=1.0, in1=last[:, 1, :],
                                                    op0=ALU.mult, op1=ALU.mult, accum_out=total[:, q:q + 1]))
                link(V.tensor_scalar(T0, SPOP, gw[:, 0:1], None, ALU.mult))
                link(V.scalar_tensor_tensor(out=T1, in0=SAGE, scalar=gw[:, 1:2], in1=T0, op0=ALU.mult, op1=ALU.add))
                link(V.tensor_tensor(T0, T1, RDEN, ALU.mult))
                link(V.tensor_scalar(Z, T0, gb[:, 0:1], None, ALU.add))
                link(V.tensor_scalar(ZNEG, Z, 0.0, None, ALU.min))
                V.scalar_tensor_tensor(out=ZABS, in0=Z, scalar=-1.0, in1=Z, op0=ALU.mult, op1=ALU.min
                                       ).then_inc(gate_in, 1)

            def setup_last_weights():
                dve.wait_ge(gate_exp, 1)
                link(V.tensor_scalar(T0, EZABS, 1.0, None, ALU.add))
                link(V.reciprocal(T1, T0))
                link(V.tensor_tensor(GATE, EZNEG, T1, ALU.mult))
                link(V.tensor_scalar(stay_[:, :], GATE, -1.0, 1.0, ALU.mult, ALU.add))
                link(V.tensor_tensor(GDIV, GATE, RDEN, ALU.mult))
                for i in range(LAST):
                    link(V.scalar_tensor_tensor(out=lw[:, i, :], in0=FIRST, scalar=float(i), in1=CNT,
                                                op0=ALU.add, op1=ALU.is_lt))
                    link(V.tensor_tensor(lw[:, i, :], lw[:, i, :], GDIV, ALU.mult))

            def short_term(g, i):
                w = lw[:, i, bass.ds(g, 1)]
                if i == 0:
                    dve.wait_ge(gathered, g * 16 + 16)
                    ins = V.tensor_scalar(short[:, :], taken[:, i, :], w, None, ALU.mult)
                else:
                    dve.wait_ge(short_part, g * LAST + i)
                    ins = V.scalar_tensor_tensor(out=short[:, :], in0=taken[:, i, :], scalar=w, in1=short[:, :],
                                                 op0=ALU.mult, op1=ALU.add)
                ins.then_inc(short_part, 1)

            def mask_and_max(s, k):
                dve.wait_ge(vsums_done, s * PAIR + PAIR)
                dve.wait_ge(gsums_done, s * PAIR + PAIR)
                dve.wait_ge(dots_done, s * PAIR + PAIR)
                V.tensor_tensor(kept[:, :], score[:, k % 2, :, :].rearrange("p t r -> p (t r)"),
                                hide[:, bass.ds(s * PROWS, PROWS)], ALU.add).then_inc(kept_ready, 1)
                dve.wait_ge(kept_ready, s + 1)
                V.tensor_reduce(pmax[:, :], kept[:, :].rearrange("p (t r) -> p t r", t=PAIR), AX.X, ALU.max
                                ).then_inc(pmax_ready, 1)

            def user_max(s):
                dve.wait_ge(pmax_turned, s + 1)
                V.tensor_reduce(umax[:, :], ps_max[0:PAIR, 0:P].rearrange("t (u c) -> t u c", c=PU), AX.X, ALU.max
                                ).then_inc(umax_ready, 1)
                dve.wait_ge(umax_ready, s + 1)
                V.tensor_scalar(nmax[:, :].rearrange("t (u c) -> t u c", c=PU),
                                umax[:, :].unsqueeze(2).broadcast_to([PAIR, TU, PU]), -1.0, None, ALU.mult
                                ).then_inc(nmax_ready, 1)

            def weights(s, k):
                dve.wait_ge(exp_done, s + 1)
                if has(s, 1):
                    dve.wait_ge(pblk_ready, s * PAIR)
                for t in range(PAIR):
                    i = (k % GP) * PAIR + t
                    V.scalar_tensor_tensor(out=wts[:, t, :], in0=ex[:, t, :], scalar=1.0,
                                           in1=decay[:, bass.ds(s * PROWS + t * ROWS, ROWS)],
                                           op0=ALU.mult, op1=ALU.mult, accum_out=wsum[:, i:i + 1]).then_inc(wts_ready, 1)

            def lay_out_sums(s):
                dve.wait_ge(wts_ready, (s - 1) * PAIR)
                V.tensor_tensor(wsum_blk[:, :, :], own[:, :].unsqueeze(1).broadcast_to([P, GP * PAIR, TU]),
                                wsum[:, :].unsqueeze(2).broadcast_to([P, GP * PAIR, TU]), ALU.mult
                                ).then_inc(wsum_ready, 1)

            def products(s, k, t):
                dve.wait_ge(query_ready, s * PAIR + t + 1)
                if has(s, 1):
                    dve.wait_ge(vsums_done, (s - 1) * PAIR + t + 1)
                V.tensor_tensor(vprod[:, t, :].rearrange("p (r d) -> p r d", d=D),
                                rows((k % GP) * PAIR + t, DOTS, DOTS + VPROD),
                                query[:, k % 2, t, :].unsqueeze(1).broadcast_to([P, VPROD, D]),
                                ALU.mult).then_inc(vprod_ready, 1)

            def dots(s, k, t, a, b):
                for r in range(a, b):
                    ins = V.scalar_tensor_tensor(out=junk_v[:, t, r, :], in0=x[:, (k % GP) * PAIR + t, r * D:(r + 1) * D],
                                                 scalar=1.0, in1=query[:, k % 2, t, :], op0=ALU.mult, op1=ALU.mult,
                                                 accum_out=score[:, k % 2, t, r:r + 1])
                if a < b == DOTS:
                    ins.then_inc(dots_done, 1)

            def finish_scales(g):
                dve.wait_ge(den_done, g)
                V.reciprocal(rden[:, :], ps_fin[:, 0:1]).then_inc(rden_ready, 1)
                dve.wait_ge(rden_ready, g)
                V.tensor_tensor(long_scale[:, :], rden[:, :], stay_[:, bass.ds(g - 1, 1)], ALU.mult
                                ).then_inc(scale_ready, 1)

            def finish_att(g):
                dve.wait_ge(wx_folded, g * GP)
                V.tensor_copy(att_t[:, :], ps_group[:, 0:P]).then_inc(att_t_ready, 1)

            def finish_user(g):
                dve.wait_ge(long_done, g)
                dve.wait_ge(short_part, g * LAST)
                dve.wait_ge(scale_ready, g)
                V.scalar_tensor_tensor(out=user[:, :], in0=ps_fin[:, 256:384], scalar=long_scale[:, :],
                                       in1=short[:, :], op0=ALU.mult, op1=ALU.add).then_inc(user_ready, 1)

            def finish_stats(g):
                dve.wait_ge(user_ready, g)
                V.bn_stats(bn[:, :], user[:, :]).then_inc(bn_ready, 1)

            def finish_moments(g):
                dve.wait_ge(bn_ready, g)
                dve.sem_inc(dve_passed, 1)
                V.bn_aggr(mv[:, :], bn[:, :]).then_inc(mv_ready, 1)

            def finish_variance(g):
                dve.wait_ge(mv_ready, g)
                V.tensor_scalar(vare[:, :], mv[:, 1:2], 1e-5, None, ALU.add).then_inc(var_ready, 1)

            def finish_centre(g):
                dve.wait_ge(mv_ready, g)
                V.scalar_tensor_tensor(out=centred[:, :], in0=user[:, :], scalar=mv[:, 0:1], in1=gam[:, :],
                                       op0=ALU.subtract, op1=ALU.mult).then_inc(centred_ready, 1)

            def finish_scale(g):
                dve.wait_ge(rstd_ready, g)
                dve.wait_ge(centred_ready, g)
                V.scalar_tensor_tensor(out=y[:, bass.ds(g - 1, 1), :].rearrange("p q d -> p (q d)"), in0=centred[:, :],
                                       scalar=rstd[:, :], in1=bet[:, :], op0=ALU.mult, op1=ALU.add
                                       ).then_inc(y_ready, 1)

            def step(g, k):
                s = g * GP + k
                fin = has(g, 1, NGROUP)
                if has(s, 1):
                    products(s - 1, k - 1, 1)
                for i in range(DOTS):
                    if i == (WEIGHTS_AT if has(s, 0) else 7) and has(s, 2):
                        if k == 2 and fin:
                            dve.wait_ge(wsum_ready, g)
                        weights(s - 2, k - 2)
                    if i == WEIGHTS_AT + 1 and k == 1 and fin:
                        lay_out_sums(s)
                    if 2 < i < 3 + LAST and k == 0 and fin and has(s, 0):
                        short_term(g - 1, i - 3)
                    if has(s, 1):
                        dots(s - 1, k - 1, 1, i, i + 1)
                if has(s, 0):
                    products(s, k, 0)
                parts = {}
                if k == 3 and fin:
                    parts = dict(zip((6, 7, 8, 9, 10, 12), (
                        finish_user, finish_stats, finish_moments, finish_variance, finish_centre, finish_scale)))
                if k == 2 and fin:
                    parts = {3: finish_scales, 11: finish_att}
                for i in range(DOTS):
                    if i == KEPT_AT and has(s, 1):
                        mask_and_max(s - 1, k - 1)
                    if i == USER_MAX_AT and has(s, 1):
                        user_max(s - 1)
                        if not has(s, 0) and fin and k == 0:
                            for j in range(LAST):
                                short_term(g - 1, j)
                    if i in parts:
                        parts[i](g)
                    if has(s, 0):
                        dots(s, k, 0, i, i + 1)

            setup_early()
            setup_decay()
            setup_gate()
            step(0, 0)
            setup_hide()
            step(0, 1)
            setup_masked_decay()
            setup_last_weights()
            steps(dve, step, NPAIR + 3, first=2)

    return nc


def kernel(**inputs):
    import numpy as _np
    import concourse.bacc as _bacc
    from concourse.bass_utils import run_bass_kernel_spmd as _run

    names = ["r_hist_items", "r_hist_mask", "r_hist_age_hours", "r_hist_popularity", "L0_rec_Wq", "L0_rec_Wk",
             "L0_rec_Wv", "L0_rec_gate_w", "L0_rec_gate_b", "L0_rec_ln_gamma", "L0_rec_ln_beta", "L0_rec_decay_alpha"]
    nc = _bacc.Bacc("TRN2", target_bir_lowering=False, num_devices=1)
    arrays, args = {}, []
    for name in names:
        a = _np.ascontiguousarray(inputs[name])
        arrays[f"in_{name}_dram"] = a
        args.append(nc.dram_tensor(f"in_{name}_dram", a.shape, mybir.dt.from_np(a.dtype), kind="ExternalInput").ap())
    out = nc.dram_tensor("out_dram", (NUSER, D), F32, kind="ExternalOutput").ap()
    build(nc, *args, out)
    r = _run(nc, [arrays], core_ids=[0])
    return r.results[0]["out_dram"]
```
